# Optimizing a Trainium2 kernel written in Bass

```python
import numpy as np
import jax
import jax.numpy as jnp

def _softmax(x, axis=-1):
    return jax.nn.softmax(x, axis=axis)

def _gelu(x):
    return jax.nn.gelu(x, approximate=True)

def _silu(x):
    return jax.nn.silu(x)

def _sigmoid(x):
    return jax.nn.sigmoid(x)

def _layernorm(x, axis=-1, eps=1e-05):
    m = jnp.mean(x, axis=axis, keepdims=True)
    v = jnp.var(x, axis=axis, keepdims=True)
    return (x - m) / jnp.sqrt(v + eps)

def _scatter_add(tgt, idx, src, axis=0):
    return tgt.at[idx].add(src)

def _segment_sum(src, seg, n):
    return jax.ops.segment_sum(src, seg, n)
kernel_name = 'mk_macaron_d1_jaxref_r4_16d556'

def setup_inputs(seed: int=0):
    np.random.seed(seed)
    _w = jnp.asarray

    def _L0_attn_setup():
        import jax, jax.numpy as jnp
        import numpy as np
        import math
        B, T, D, H = (2, 512, 256, 16)
        DH = D // H

        def rotate_half(x):
            x1 = x[..., ::2]
            x2 = x[..., 1::2]
            return jnp.stack((-x2, x1), axis=-1).reshape(x.shape)
        key = jax.random.key(seed)
        k1, k2, k3 = jax.random.split(key, 3)
        x = jax.random.normal(k1, (B, T, D), dtype=jnp.float32)
        Wqkv = jax.random.normal(k2, (3 * D, D), dtype=jnp.float32) * (1.0 / math.sqrt(D))
        Wo = jax.random.normal(k3, (D, D), dtype=jnp.float32) * (1.0 / math.sqrt(D))
        return {'x': x, 'Wqkv': Wqkv, 'Wo': Wo}
    _L0_attn_in = _L0_attn_setup()

    def _L0_ffn_setup():
        import jax, jax.numpy as jnp
        import numpy as np
        TOP_K = 2
        key = jax.random.key(seed)
        ks = jax.random.split(key, 6)
        B, S, D, E = (8, 1024, 256, 8)
        s = 1.0 / np.sqrt(D)
        return {'x': jax.random.normal(ks[0], (B, S, D), dtype=jnp.float32), 'Wr': jax.random.normal(ks[1], (D, E), dtype=jnp.float32) * s, 'br': jnp.zeros((E,), dtype=jnp.float32), 'W1': jax.random.normal(ks[2], (E, D, D), dtype=jnp.float32) * s, 'b1': jnp.zeros((E, D), dtype=jnp.float32), 'W2': jax.random.normal(ks[3], (E, D, D), dtype=jnp.float32) * s, 'b2': jnp.zeros((E, D), dtype=jnp.float32)}
    _L0_ffn_in = _L0_ffn_setup()
    _d = {'L0_attn_x': _L0_attn_in['x'], 'L0_attn_Wqkv': _L0_attn_in['Wqkv'], 'L0_attn_Wo': _L0_attn_in['Wo'], 'L0_ffn_Wr': _L0_ffn_in['Wr'], 'L0_ffn_br': _L0_ffn_in['br'], 'L0_ffn_W1': _L0_ffn_in['W1'], 'L0_ffn_b1': _L0_ffn_in['b1'], 'L0_ffn_W2': _L0_ffn_in['W2'], 'L0_ffn_b2': _L0_ffn_in['b2']}
    _x0 = _d['L0_attn_x']
    _d['L0_attn_x'] = jax.random.normal(jax.random.fold_in(jax.random.key(seed), 1), (32, 512, 256), dtype=_x0.dtype)
    del _x0
    return _d

def reference(L0_attn_x, L0_attn_Wqkv, L0_attn_Wo, L0_ffn_Wr, L0_ffn_br, L0_ffn_W1, L0_ffn_b1, L0_ffn_W2, L0_ffn_b2):

    def _L0_attn_ref(x, Wqkv, Wo):
        import jax, jax.numpy as jnp
        import numpy as np
        import math
        B, T, D, H = (2, 512, 256, 16)
        DH = D // H

        def rotate_half(x):
            x1 = x[..., ::2]
            x2 = x[..., 1::2]
            return jnp.stack((-x2, x1), axis=-1).reshape(x.shape)
        b, t, d = x.shape
        pos = jnp.arange(t, dtype=jnp.float32)
        freqs = jnp.exp(-math.log(10000.0) * jnp.arange(0, DH, 2, dtype=jnp.float32) / DH)
        angles = pos[:, None] * freqs[None, :]
        angles = jnp.repeat(angles, 2, axis=-1)
        sin = jnp.sin(angles)[None, None, :, :]
        cos = jnp.cos(angles)[None, None, :, :]
        qkv = x @ Wqkv.T
        q, k, v = jnp.split(qkv, 3, axis=-1)
        q = q.reshape(b, t, H, DH).transpose(0, 2, 1, 3)
        k = k.reshape(b, t, H, DH).transpose(0, 2, 1, 3)
        v = v.reshape(b, t, H, DH).transpose(0, 2, 1, 3)
        q = cos * q + rotate_half(q) * sin
        k = cos * k + rotate_half(k) * sin
        scores = jnp.einsum('bhqd,bhkd->bhqk', q, k) / math.sqrt(DH)
        causal = jnp.tril(jnp.ones((t, t), dtype=bool))
        scores = jnp.where(causal, scores, -jnp.inf)
        attn = jax.nn.softmax(scores, axis=-1)
        out = jnp.einsum('bhqk,bhkd->bhqd', attn, v)
        out = out.transpose(0, 2, 1, 3).reshape(b, t, d)
        return out @ Wo.T

    def _L0_ffn_ref(x, Wr, br, W1, b1, W2, b2):
        import jax, jax.numpy as jnp
        import numpy as np
        TOP_K = 2
        k = TOP_K
        scores0 = x[:, 0, :] @ Wr + br
        _, idx = jax.lax.top_k(scores0, k)
        W1g, b1g = (W1[idx], b1[idx])
        W2g, b2g = (W2[idx], b2[idx])
        h = jnp.einsum('bsd,bkde->bkse', x, W1g) + b1g[:, :, None, :]
        h = jax.nn.gelu(h, approximate=False)
        o = jnp.einsum('bkse,bkef->bksf', h, W2g) + b2g[:, :, None, :]
        return jnp.sum(o, axis=1) / k
    x = L0_attn_x
    x = x + 0.5 * _L0_ffn_ref(_layernorm(x, axis=-1), L0_ffn_Wr, L0_ffn_br, L0_ffn_W1, L0_ffn_b1, L0_ffn_W2, L0_ffn_b2)
    x = x + _L0_attn_ref(_layernorm(x, axis=-1), L0_attn_Wqkv, L0_attn_Wo)
    x = x + 0.5 * _L0_ffn_ref(_layernorm(x, axis=-1), L0_ffn_Wr, L0_ffn_br, L0_ffn_W1, L0_ffn_b1, L0_ffn_W2, L0_ffn_b2)
    return x

_drawn_inputs = setup_inputs


def setup_inputs(seed=0):
    import zlib

    import numpy as np

    out = dict(_drawn_inputs(seed))
    spreads = {'L0_ffn_br': (0.0, 0.1), 'L0_ffn_b1': (0.0, 0.1), 'L0_ffn_b2': (0.0, 0.1)}
    factors = {}
    for name, (base, spread) in spreads.items():
        noise = np.random.default_rng([zlib.crc32(name.encode()), seed]).standard_normal(out[name].shape)
        drawn = base * np.exp(spread * noise) if base else spread * noise
        out[name] = jnp.asarray(drawn.astype(out[name].dtype))
    for name, factor in factors.items():
        out[name] = (out[name] * factor).astype(out[name].dtype)
    return out
```

```python
from contextlib import ExitStack

import concourse.bass as bass
from concourse import mybir

ALU = mybir.AluOpType
ACT = mybir.ActivationFunctionType
AX_X = mybir.AxisListType.X
F32 = mybir.dt.float32
F16 = mybir.dt.float16
BF16 = mybir.dt.bfloat16
I32 = mybir.dt.int32
U32 = mybir.dt.uint32

P = 128
B, T, D = 32, 512, 256
E, TOP_K = 8, 2
NT = T // P
NC = D // P
EPS = 1e-5
H = 16
DH = D // H
GH = 4
ST_BANK = (0, 1, 2, 0, 1, 2, 0, 1, 2, 1)
HALF = 0.5


class At:

    def __init__(self, k, c):
        self.k, self.c = k, c

    def __add__(self, n):
        return At(self.k, self.c + n)

    @property
    def par(self):
        return self.c % 2

    @property
    def half(self):
        return self.k + self.c // 2

    @property
    def b(self):
        return self.k * 2 + self.c


def wait(eng, sem, value):
    if isinstance(value, int) and value <= 0:
        return
    eng.wait_ge(sem, value)


def hold(sp, issue, sem, value):
    if isinstance(value, int) and value <= 0:
        return
    sp.wait_ge(sem, value)
    sp.sem_inc(issue, 1)


class Tables:
    pass


class Split:

    def __init__(self, hi, lo):
        self.hi, self.lo = hi, lo


TERMS = (("hi", "hi"), ("lo", "hi"), ("hi", "lo"))


def over_samples(eng, step):
    step(At(0, 0), first=True, last=False)
    step(At(0, 1), first=False, last=False)
    with eng.Fori(0, (B - 4) // 2) as k:
        step(At(k, 2), first=False, last=False)
        step(At(k, 3), first=False, last=False)
    step(At(0, B - 2), first=False, last=False)
    step(At(0, B - 1), first=False, last=True)


def layernorm_stats(nc, dve, stats_step, stats_done, b, x, stats, pair, ve):
    for t in range(NT):
        ins = nc.vector.bn_stats(stats[:, t, :], x[:, t, :])
    ins.then_inc(stats_step, 1)
    dve.wait_ge(stats_step, 3 * b + 1)
    nc.vector.tensor_tensor(pair[:, 0, :], stats[:, :, 1], stats[:, :, 4], ALU.add)
    nc.vector.tensor_tensor(pair[:, 1, :], stats[:, :, 1], stats[:, :, 4], ALU.subtract)
    nc.vector.tensor_tensor(pair[:, 2, :], stats[:, :, 2], stats[:, :, 5], ALU.add).then_inc(stats_step, 1)
    dve.wait_ge(stats_step, 3 * b + 2)
    nc.vector.tensor_scalar(ve[:, 1, :], pair[:, 0, :], -0.5, None, ALU.mult)
    nc.vector.tensor_tensor(pair[:, 3, :], pair[:, 1, :], pair[:, 1, :], ALU.mult)
    nc.vector.tensor_scalar(pair[:, 4, :], pair[:, 2, :], 1.0 / D, EPS, ALU.mult, ALU.add).then_inc(stats_step, 1)
    dve.wait_ge(stats_step, 3 * b + 3)
    nc.vector.scalar_tensor_tensor(out=ve[:, 0, :], in0=pair[:, 3, :], scalar=0.25, in1=pair[:, 4, :],
                                   op0=ALU.mult, op1=ALU.add).then_inc(stats_done, 1)


def build_tables(nc, tab, W1, W2, b1T, WqkvT, WoT):
    with ExitStack() as ctx:
        sb = lambda n, s, d: ctx.enter_context(nc.sbuf_tensor(n, s, d))
        sem = lambda n: ctx.enter_context(nc.semaphore(n))
        w1f = sb("w1_stage", [P, E, NC * D], F32)
        w2f = sb("w2_stage", [P, E, NC * D], F32)
        qkvf = sb("qkv_stage", [P, NC, 3 * D], F32)
        wof = sb("wo_stage", [P, NC, D], F32)
        loaded = {n: sem(f"{n}_loaded") for n in ("w1", "w2", "b1", "qkv", "wo")}
        ident_zeroed = sem("ident_zeroed")
        w1_hi, w2_hi, small_hi, tables_done = sem("w1_hi"), sem("w2_hi"), sem("small_hi"), sem("tables_done")
        block = ctx.enter_context(nc.Block())

        @block.sync
        def _(sp):
            sp.dma_start(w1f[:].rearrange("p e (c n) -> p e c n", c=NC),
                         W1.rearrange("e (c p) n -> p e c n", p=P)).then_inc(loaded["w1"], 16)
            sp.dma_start(w2f[:].rearrange("p e (c n) -> p e c n", c=NC),
                         W2.rearrange("e (c p) n -> p e c n", p=P)).then_inc(loaded["w2"], 16)
            sp.dma_start(tab.b1[:], b1T).then_inc(loaded["b1"], 16)
            sp.wait_ge(loaded["b1"], 16)

        @block.scalar
        def _(act):
            act.dma_start(qkvf[:], WqkvT.rearrange("(c p) n -> p c n", p=P)).then_inc(loaded["qkv"], 16)
            act.dma_start(wof[:], WoT.rearrange("(c p) n -> p c n", p=P)).then_inc(loaded["wo"], 16)
            act.wait_ge(loaded["w1"], 16)
            nc.scalar.activation(tab.w1.hi[:], w1f[:], ACT.Copy).then_inc(w1_hi, 1)
            act.wait_ge(loaded["qkv"], 16)
            nc.scalar.activation(tab.qkv.hi[:], qkvf[:], ACT.Copy).then_inc(small_hi, 1)
            act.wait_ge(loaded["wo"], 16)
            nc.scalar.activation(tab.wo.hi[:], wof[:], ACT.Copy).then_inc(small_hi, 1)

        @block.vector
        def _(dve):
            dve.wait_ge(loaded["w2"], 16)
            nc.vector.tensor_copy(tab.w2.hi[:], w2f[:]).then_inc(w2_hi, 1)
            dve.wait_ge(w1_hi, 1)
            nc.vector.tensor_tensor(tab.w1.lo[:], w1f[:], tab.w1.hi[:], ALU.subtract).then_inc(tables_done, 1)
            dve.wait_ge(w2_hi, 1)
            nc.vector.tensor_tensor(tab.w2.lo[:], w2f[:], tab.w2.hi[:], ALU.subtract).then_inc(tables_done, 1)
            dve.wait_ge(small_hi, 2)
            nc.vector.tensor_tensor(tab.qkv.lo[:], qkvf[:], tab.qkv.hi[:], ALU.subtract).then_inc(tables_done, 1)
            nc.vector.tensor_tensor(tab.wo.lo[:], wof[:], tab.wo.hi[:], ALU.subtract).then_inc(tables_done, 1)
            dve.wait_ge(tables_done, 8)

        @block.gpsimd
        def _(pool):
            nc.gpsimd.memset(tab.ident[:], 0.0).then_inc(ident_zeroed, 1)
            nc.gpsimd.memset(tab.minus_half[:], -0.5).then_inc(tables_done, 1)
            nc.gpsimd.memset(tab.quarter[:], HALF / TOP_K).then_inc(tables_done, 1)
            nc.gpsimd.memset(tab.identb[:], 0.0).then_inc(ident_zeroed, 1)
            nc.gpsimd.memset(tab.mask[:], 0.0).then_inc(ident_zeroed, 1)
            pool.wait_ge(ident_zeroed, 3)
            nc.gpsimd.affine_select(out=tab.ident[:], in_=tab.ident[:], compare_op=ALU.not_equal, fill=1.0,
                                    base=0, pattern=[[-1, P]], channel_multiplier=1).then_inc(tables_done, 1)
            nc.gpsimd.affine_select(out=tab.identb[:], in_=tab.identb[:], compare_op=ALU.not_equal, fill=1.0,
                                    base=0, pattern=[[-1, P]], channel_multiplier=1).then_inc(ident_zeroed, 1)
            nc.gpsimd.affine_select(out=tab.mask[:], in_=tab.mask[:], compare_op=ALU.is_ge, fill=-1e30,
                                    base=0, pattern=[[-1, P]], channel_multiplier=1).then_inc(tables_done, 1)
            pool.wait_ge(ident_zeroed, 4)


def ffn_phase(nc, tag, tab, src, dst, Wr, br, b2):
    with ExitStack() as ctx:
        sb = lambda n, s, d: ctx.enter_context(nc.sbuf_tensor(f"{tag}_{n}", s, d))
        pb = lambda n, s, d: ctx.enter_context(nc.psum_tensor(f"{tag}_{n}", s, d))
        sem = lambda n: ctx.enter_context(nc.semaphore(f"{tag}_{n}"))

        row = sb("row", [B, D], F32)
        row_n = sb("row_n", [B, D], F32)
        row_stats = sb("row_stats", [B, 6], F32)
        row_mv = sb("row_mv", [B, 2], F32)
        row_ve = sb("row_ve", [B, 2], F32)
        row_rstd = sb("row_rstd", [B, 1], F32)
        rowT = sb("rowT", [P, NC, B], F32)
        wr = sb("wr", [P, NC, E], F32)
        brb = sb("brb", [B, E], F32)
        logits = sb("logits", [B, E], F32)
        top = sb("top", [B, 8], F32)
        top_i = sb("top_i", [B, 8], U32)
        routes = sb("routes", [1, B * TOP_K], U32)
        x = [sb(f"x{i}", [P, NT, D], F32) for i in range(2)]
        xn = sb("xn", [P, NT, D], F32)
        stats = sb("stats", [P, NT, 6], F32)
        pair = sb("pair", [P, 5, NT], F32)
        ve = sb("ve", [P, 2, NT], F32)
        rstd = sb("rstd", [P, NT], F32)
        xT = [Split(sb(f"xThi{i}", [P, NC, T], F16), sb(f"xTlo{i}", [P, NC, T], F16)) for i in range(2)]
        w1 = [Split(sb(f"w1hi{i}", [P, TOP_K, NC * D], F16), sb(f"w1lo{i}", [P, TOP_K, NC * D], F16)) for i in range(2)]
        w2 = [Split(sb(f"w2hi{i}", [P, TOP_K, NC * D], F16), sb(f"w2lo{i}", [P, TOP_K, NC * D], F16)) for i in range(2)]
        b1s = [sb(f"b1s{i}", [P, TOP_K, NC], F32) for i in range(2)]
        b2s = [sb(f"b2s{i}", [P, TOP_K, D], F32) for i in range(2)]
        b2sum = sb("b2sum", [P, D], F32)
        b2q = sb("b2q", [P, D], F32)
        h32 = [sb(f"h32_{i}", [P, T], F32) for i in range(4)]
        h = [Split(sb(f"hhi{i}", [P, 4, T], F16), sb(f"hlo{i}", [P, 4, T], F16)) for i in range(2)]
        res = [sb(f"res{i}", [P, NT, D], F32) for i in range(2)]
        xT_ps = [pb(f"xT_ps{c}", [P, T], F32) for c in range(NC)]
        h_ps = [pb(f"h_ps{j}", [P, T], F32) for j in range(4)]
        y_ps = [pb(f"y_ps{j}", [P, 2, D], F32) for j in range(2)]

        row_loaded, wr_loaded, routes_loaded = sem("row_loaded"), sem("wr_loaded"), sem("routes_loaded")
        r_stats, r_rstd, r_norm = sem("r_stats"), sem("r_rstd"), sem("r_norm")
        r_T, r_Tcopied, r_logits, r_top = sem("r_T"), sem("r_Tcopied"), sem("r_logits"), sem("r_top")
        x_loaded = [sem(f"x_loaded{i}") for i in range(2)]
        w1_loaded = [sem(f"w1_loaded{i}") for i in range(2)]
        w2_loaded = [sem(f"w2_loaded{i}") for i in range(2)]
        b2_loaded = [sem(f"b2_loaded{i}") for i in range(2)]
        stored = [sem(f"stored{i}") for i in range(2)]
        norm_starts, issue = sem("norm_starts"), sem("issue")
        stats_step, stats_done, rstd_done, xn_done = sem("stats_step"), sem("stats_done"), sem("rstd_done"), sem("xn_done")
        xT_done, xT_hi, xT_lo = sem("xT_done"), sem("xT_hi"), sem("xT_lo")
        h_done, gelu_done, h_lo, y_done = sem("h_done"), sem("gelu_done"), sem("h_lo"), sem("y_done")
        b2_step, res_ready, out_done = sem("b2_step"), sem("res_ready"), sem("out_done")
        block = ctx.enter_context(nc.Block())

        src_v = src.rearrange("b (p t) d -> b p (t d)", t=NT)
        dst_v = dst.rearrange("b (p t) d -> b p (t d)", t=NT)

        def load_x(sp, s):
            hold(sp, issue, xn_done, NT * s.b - NT)
            hold(sp, issue, res_ready, s.b - 1)
            sp.dma_start(x[s.par][:].rearrange("p t d -> p (t d)"),
                         src_v[bass.ds(s.b, 1)].rearrange("b p n -> p (b n)")).then_inc(x_loaded[s.par], 16)

        def route(sp, s, k):
            return sp.value_load(routes[0:1, bass.ds(s.b * TOP_K + k, 1)], min_val=0, max_val=E - 1)

        @block.sync
        def _(sp):
            sp.dma_start(row[:], src[:, 0, :]).then_inc(row_loaded, 16)
            sp.dma_start(wr[:], Wr.rearrange("(c p) e -> p c e", p=P)).then_inc(wr_loaded, 16)
            sp.dma_start(brb[:], br.rearrange("(a e) -> a e", a=1).broadcast_to([B, E])).then_inc(wr_loaded, 16)
            load_x(sp, At(0, 0))
            load_x(sp, At(0, 1))
            sp.wait_ge(r_top, 2)
            sp.dma_start(routes[:].rearrange("a (b k) -> a b k", k=TOP_K), top_i[:, 0:TOP_K]).then_inc(routes_loaded, 16)
            sp.wait_ge(routes_loaded, 16)

            def load_first(s):
                e = [route(sp, s, k) for k in range(TOP_K)]
                hold(sp, issue, h_done, 4 * s.b - 4)
                hold(sp, issue, gelu_done, 8 * s.b - 8)
                for k in range(TOP_K):
                    sp.dma_start(w1[s.par].hi[:, k, :], tab.w1.hi[:, bass.ds(e[k], 1), :]).then_inc(w1_loaded[s.par], 16)
                    sp.dma_start(w1[s.par].lo[:, k, :], tab.w1.lo[:, bass.ds(e[k], 1), :]).then_inc(w1_loaded[s.par], 16)
                    sp.dma_start(b1s[s.par][:, k, :], tab.b1[:, bass.ds(e[k], 1), :]).then_inc(w1_loaded[s.par], 16)
                hold(sp, issue, res_ready, s.b - 1)
                for k in range(TOP_K):
                    sp.dma_start(b2s[s.par][:, k, :], b2[bass.ds(e[k], 1), :].broadcast_to([P, D])).then_inc(b2_loaded[s.par], 16)
                return e

            def load_second(s, e):
                hold(sp, issue, y_done, 2 * s.b - 2)
                for k in range(TOP_K):
                    sp.dma_start(w2[s.par].hi[:, k, :], tab.w2.hi[:, bass.ds(e[k], 1), :]).then_inc(w2_loaded[s.par], 16)
                    sp.dma_start(w2[s.par].lo[:, k, :], tab.w2.lo[:, bass.ds(e[k], 1), :]).then_inc(w2_loaded[s.par], 16)

            load_second(At(0, 0), load_first(At(0, 0)))

            def step(s, last_x):
                e = load_first(s + 1)
                if not last_x:
                    load_x(sp, s + 2)
                load_second(s + 1, e)
                if not (isinstance(s.b, int) and s.b == 0):
                    store(s + -1)

            def store(s):
                hold(sp, issue, out_done, 2 * s.b + 2)
                sp.dma_start(dst_v[bass.ds(s.b, 1)].rearrange("b p n -> p (b n)"),
                             res[s.par][:].rearrange("p t d -> p (t d)")).then_inc(stored[s.par], 16)

            step(At(0, 0), False)
            step(At(0, 1), False)
            with sp.Fori(0, (B - 4) // 2) as k:
                step(At(k, 2), False)
                step(At(k, 3), False)
            step(At(0, B - 2), True)
            store(At(0, B - 2))
            store(At(0, B - 1))
            for i in range(2):
                hold(sp, issue, stored[i], 16 * (B // 2))

        @block.gpsimd
        def _(pool):
            pool.wait_ge(r_stats, 4)
            nc.gpsimd.tensor_tensor(row_rstd[:], row_ve[:, 0:1], tab.minus_half[0:B, 0:1], ALU.pow).then_inc(r_rstd, 1)
            pool.wait_ge(r_rstd, 1)
            nc.gpsimd.tensor_scalar(row_n[:], row[:], row_ve[:, 1:2], row_rstd[:, 0:1], ALU.add, ALU.mult).then_inc(r_norm, 1)

            def norm(s):
                pool.wait_ge(stats_done, s.b + 1)
                nc.gpsimd.tensor_tensor(rstd[:], ve[:, 0, :], tab.minus_half[:, 0:NT], ALU.pow).then_inc(rstd_done, 1)
                wait(pool, xT_done, NC * s.b)
                pool.wait_ge(rstd_done, s.b + 1)
                pool.sem_inc(norm_starts, 1)
                for t in range(NT):
                    nc.gpsimd.tensor_scalar(xn[:, t, :], x[s.par][:, t, :], ve[:, 1, t:t + 1], rstd[:, t:t + 1],
                                            ALU.add, ALU.mult).then_inc(xn_done, 1)

            def residual(s):
                pool.wait_ge(b2_loaded[s.par], 16 * TOP_K * (s.half + 1))
                pool.wait_ge(x_loaded[s.par], 16 * (s.half + 1))
                wait(pool, stored[s.par], 16 * s.half)
                nc.gpsimd.tensor_tensor(b2sum[:], b2s[s.par][:, 0, :], b2s[s.par][:, 1, :], ALU.add).then_inc(b2_step, 1)
                pool.wait_ge(b2_step, 2 * s.b + 1)
                nc.gpsimd.tensor_tensor(b2q[:], b2sum[:], tab.quarter[:], ALU.mult).then_inc(b2_step, 1)
                pool.wait_ge(b2_step, 2 * s.b + 2)
                nc.gpsimd.tensor_tensor(res[s.par][:], x[s.par][:],
                                        b2q[:].rearrange("p (t d) -> p t d", t=1).broadcast_to([P, NT, D]),
                                        ALU.add).then_inc(res_ready, 1)

            norm(At(0, 0))

            def step(s, first, last):
                if not last:
                    norm(s + 1)
                residual(s)

            over_samples(pool, step)

        @block.vector
        def _(dve):
            dve.wait_ge(row_loaded, 16)
            nc.vector.bn_stats(row_stats[:], row[:]).then_inc(r_stats, 1)
            dve.wait_ge(r_stats, 1)
            nc.vector.bn_aggr(row_mv[:], row_stats[:]).then_inc(r_stats, 1)
            dve.wait_ge(r_stats, 2)
            nc.vector.tensor_scalar(row_ve[:, 0:1], row_mv[:, 1:2], EPS, None, ALU.add).then_inc(r_stats, 1)
            nc.vector.tensor_scalar(row_ve[:, 1:2], row_mv[:, 0:1], -1.0, None, ALU.mult).then_inc(r_stats, 1)
            dve.wait_ge(r_T, 1)
            nc.vector.tensor_copy(rowT[:].rearrange("p c b -> p (c b)"), xT_ps[0][:, 0:NC * B]).then_inc(r_Tcopied, 1)
            dve.wait_ge(r_logits, 1)
            dve.wait_ge(wr_loaded, 32)
            nc.vector.tensor_tensor(logits[:], xT_ps[1][0:B, 0:E], brb[:], ALU.add).then_inc(r_Tcopied, 1)
            dve.wait_ge(r_Tcopied, 2)
            nc.vector.max(top[:], logits[:]).then_inc(r_top, 1)
            dve.wait_ge(r_top, 1)
            nc.vector.max_index(top_i[:], top[:], logits[:]).then_inc(r_top, 1)

            def norm_stats(s):
                dve.wait_ge(x_loaded[s.par], 16 * (s.half + 1))
                wait(dve, xn_done, NT * s.b)
                layernorm_stats(nc, dve, stats_step, stats_done, s.b, x[s.par], stats, pair, ve)

            def xT_low(s):
                for c in range(NC):
                    dve.wait_ge(xT_hi, NC * s.b + c + 1)
                    nc.vector.tensor_tensor(xT[s.par].lo[:, c, :], xT_ps[c][:], xT[s.par].hi[:, c, :],
                                            ALU.subtract).then_inc(xT_lo, 1)

            norm_stats(At(0, 0))
            xT_low(At(0, 0))

            def step(s, first, last):
                if not last:
                    norm_stats(s + 1)
                for j in range(4):
                    dve.wait_ge(gelu_done, 8 * s.b + 2 * j + 2)
                    wait(dve, y_done, 2 * s.b - 2)
                    nc.vector.tensor_tensor(h[s.par].lo[:, j, :], h32[j][:], h[s.par].hi[:, j, :],
                                            ALU.subtract).then_inc(h_lo, 1)
                if not last:
                    xT_low(s + 1)
                if not first:
                    output(s + -1)

            def output(s):
                dve.wait_ge(res_ready, s.b + 1)
                for g in range(2):
                    dve.wait_ge(y_done, 2 * s.b + g + 1)
                    r = res[s.par][:, 2 * g:2 * g + 2, :]
                    nc.vector.scalar_tensor_tensor(out=r, in0=y_ps[g][:], scalar=HALF / TOP_K, in1=r,
                                                   op0=ALU.mult, op1=ALU.add).then_inc(out_done, 1)

            over_samples(dve, step)
            output(At(0, B - 1))

        @block.scalar
        def _(act):
            def xT_high(s):
                for c in range(NC):
                    act.wait_ge(xT_done, NC * s.b + c + 1)
                    wait(act, h_done, 4 * s.b - 4)
                    nc.scalar.activation(xT[s.par].hi[:, c, :], xT_ps[c][:], ACT.Copy).then_inc(xT_hi, 1)

            xT_high(At(0, 0))

            def step(s, first, last):
                act.wait_ge(w1_loaded[s.par], 96 * (s.half + 1))
                wait(act, y_done, 2 * s.b - 2)
                for j in range(4):
                    act.wait_ge(h_done, 4 * s.b + j + 1)
                    wait(act, h_lo, 4 * s.b + j - 3)
                    bias = b1s[s.par][:, j // 2, j % 2:j % 2 + 1]
                    nc.scalar.activation(h32[j][:], h_ps[j][:], ACT.Gelu, bias=bias).then_inc(gelu_done, 1)
                    nc.scalar.activation(h[s.par].hi[:, j, :], h_ps[j][:], ACT.Gelu, bias=bias).then_inc(gelu_done, 1)
                if not last:
                    xT_high(s + 1)

            over_samples(act, step)

        @block.tensor
        def _(pe):
            pe.wait_ge(r_norm, 1)
            for c in range(NC):
                ins = nc.tensor.transpose(xT_ps[0][:, c * B:(c + 1) * B], row_n[:, c * P:(c + 1) * P], tab.ident[0:B, 0:B])
            ins.then_inc(r_T, 1)
            pe.wait_ge(r_Tcopied, 1)
            pe.wait_ge(wr_loaded, 32)
            for c in range(NC):
                ins = nc.tensor.matmul(xT_ps[1][0:B, 0:E], rowT[:, c, :], wr[:, c, :], start=(c == 0), stop=(c == NC - 1))
            ins.then_inc(r_logits, 1)
            pe.wait_ge(r_Tcopied, 2)

            def transposes(s):
                pe.wait_ge(xn_done, NT * (s.b + 1))
                wait(pe, xT_lo, NC * s.b)
                for c in range(NC):
                    for t in range(NT):
                        ins = nc.tensor.transpose(xT_ps[c][:, t * P:(t + 1) * P], xn[:, t, c * P:(c + 1) * P], tab.ident[:])
                    ins.then_inc(xT_done, 1)

            def times_w1(s):
                pe.wait_ge(xT_lo, NC * (s.b + 1))
                pe.wait_ge(w1_loaded[s.par], 96 * (s.half + 1))
                for j in range(4):
                    wait(pe, gelu_done, 8 * s.b + 2 * j - 6)
                    n = 0
                    for c in range(NC):
                        for wp, xp in TERMS:
                            w = (w1[s.par].hi if wp == "hi" else w1[s.par].lo)[:, j // 2, c * D + (j % 2) * P:c * D + (j % 2) * P + P]
                            v = (xT[s.par].hi if xp == "hi" else xT[s.par].lo)[:, c, :]
                            ins = nc.tensor.matmul(h_ps[j][:], w, v, start=(n == 0), stop=(n == 3 * NC - 1))
                            n += 1
                    ins.then_inc(h_done, 1)

            def times_w2(s):
                pe.wait_ge(w2_loaded[s.par], 64 * (s.half + 1))
                pe.wait_ge(h_lo, 4 * (s.b + 1))
                for t in range(NT):
                    if t % 2 == 0:
                        wait(pe, out_done, 2 * s.b + t // 2 - 1)
                    n = 0
                    for j in range(4):
                        for hp, wp in TERMS:
                            v = (h[s.par].hi if hp == "hi" else h[s.par].lo)[:, j, t * P:(t + 1) * P]
                            w = (w2[s.par].hi if wp == "hi" else w2[s.par].lo)[:, j // 2, (j % 2) * D:(j % 2) * D + D]
                            ins = nc.tensor.matmul(y_ps[t // 2][:, t % 2, :], v, w, start=(n == 0), stop=(n == 11))
                            n += 1
                    if t % 2:
                        ins.then_inc(y_done, 1)

            transposes(At(0, 0))

            def step(s, first, last):
                times_w1(s)
                if not last:
                    transposes(s + 1)
                if not first:
                    times_w2(s + -1)

            over_samples(pe, step)
            times_w2(At(0, B - 1))


def attention_phase(nc, tab, src, dst, cos, sin):
    with ExitStack() as ctx:
        sb = lambda n, s, d: ctx.enter_context(nc.sbuf_tensor(f"at_{n}", s, d))
        pb = lambda n, s, d: ctx.enter_context(nc.psum_tensor(f"at_{n}", s, d))
        sem = lambda n: ctx.enter_context(nc.semaphore(f"at_{n}"))

        cos_t, sin_t = sb("cos", [P, T], F32), sb("sin", [P, T], F32)
        zeros = sb("zeros", [H // 2, T], F16)
        ones = sb("ones", [H // 2, T], F16)
        x = sb("x", [P, NT, D], F32)
        xn = sb("xn", [P, NT, D], F32)
        stats = sb("stats", [P, NT, 6], F32)
        pair = sb("pair", [P, 5, NT], F32)
        ve = sb("ve", [P, 2, NT], F32)
        rstd = sb("rstd", [P, NT], F32)
        xT = Split(sb("xThi", [P, NC, T], F16), sb("xTlo", [P, NC, T], F16))
        swapped = [sb(f"swapped{i}", [P, T], F32) for i in range(2)]
        by_cos = [sb(f"by_cos{i}", [P, T], F32) for i in range(2)]
        by_sin = [sb(f"by_sin{i}", [P, T], F32) for i in range(2)]
        rotated = [sb(f"rotated{i}", [P, T], F32) for i in range(2)]
        qk = Split(sb("qk_hi", [P, 4, T], F16), sb("qk_lo", [P, 4, T], F16))
        q_stack = [sb(f"q_stack{i}", [P, H, T], F16) for i in range(2)]
        k_stack = [sb(f"k_stack{i}", [P, H // 2, T], F16) for i in range(2)]
        v = [sb(f"v{i}", [P, NT, H, 2 * DH], F32) for i in range(2)]
        mx = [sb(f"mx{i}", [P, NT, GH], F32) for i in range(2)]
        mneg = [sb(f"mneg{i}", [GH, T], F16) for i in range(2)]
        probs = sb("probs", [P, 10, T], F32)
        o32 = sb("o32", [P, T], F32)
        inverse = sb("inverse", [P, NT * GH], F32)
        on = [sb(f"on{i}", [P, NT, D], F32) for i in range(2)]
        oT = Split(sb("oT_hi", [P, NC, T], F16), sb("oT_lo", [P, NC, T], F16))
        res = [sb(f"res{i}", [P, NT, D], F32) for i in range(2)]
        st_ps = [pb(f"st_ps{i}", [P, T], F32) for i in range(3)]
        mx_ps = [pb(f"mx_ps{i}", [P, T], F32) for i in range(2)]
        pv_ps = pb("pv_ps", [P, T], F32)
        x_ps = [pb(f"x_ps{i}", [P, T], F32) for i in range(2)]
        image = nc.dram_tensor("qk_image", (4, D, T), F16, kind="Internal").ap()

        tables_loaded, stacks_zeroed, stacks_set, consts_set = sem("tables_loaded"), sem("stacks_zeroed"), sem("stacks_set"), sem("consts_set")
        x_loaded, q_written, k_written, q_stacked = sem("x_loaded"), sem("q_written"), sem("k_written"), sem("q_stacked")
        k_stacked, stats_step, stats_done, rstd_done = sem("k_stacked"), sem("stats_step"), sem("stats_done"), sem("rstd_done")
        xn_starts, xn_done, xT_done, xT_hi = sem("xn_starts"), sem("xn_done"), sem("xT_done"), sem("xT_hi")
        xT_lo, qk_done, rope_in, sin_done = sem("xT_lo"), sem("qk_done"), sem("rope_in"), sem("sin_done")
        rope_done, qk_hi, qk_lo, v_done = sem("rope_done"), sem("qk_hi"), sem("qk_lo"), sem("v_done")
        v_copied, mx_done, max_done, mt_done = sem("v_copied"), sem("mx_done"), sem("max_done"), sem("mt_done")
        mt_copied, st_done, exp_done, masked = sem("mt_copied"), sem("st_done"), sem("exp_done"), sem("masked")
        pv_done, o_copied, o_turned, inverse_done = sem("pv_done"), sem("o_copied"), sem("o_turned"), sem("inverse_done")
        on_done, oT_done, oT_hi, oT_lo = sem("on_done"), sem("oT_done"), sem("oT_hi"), sem("oT_lo")
        o_done, res_done, issue, mask_starts = sem("o_done"), sem("res_done"), sem("issue"), sem("mask_starts")
        res_loaded = [sem(f"res_loaded{i}") for i in range(2)]
        stored = [sem(f"stored{i}") for i in range(2)]
        rows_set = [sem(f"rows_set{i}") for i in range(2)]
        block = ctx.enter_context(nc.Block())

        src_v = src.rearrange("b (t p) d -> b p t d", p=P)
        dst_v = dst.rearrange("b (t p) d -> b p t d", p=P)

        def schedule(eng, slot):
            for g in (2, 3):
                slot(At(0, -2), g)
            for c in range(-1, 3):
                for g in range(4):
                    slot(At(0, c), g)
            with eng.Fori(0, (B - 6) // 2) as k:
                for c in (3, 4):
                    for g in range(4):
                        slot(At(k, c), g)
            for c in range(B - 3, B + 1):
                for g in range(4):
                    slot(At(0, c), g)
            slot(At(0, B + 1), 0)

        def group(G):
            return not isinstance(G, int) or 0 <= G < B * 4

        def sample(s):
            return not isinstance(s.b, int) or 0 <= s.b < B

        def of_group(s, g, lag):
            return s + (g - lag) // 4, (g - lag) % 4

        @block.sync
        def _(sp):
            sp.dma_start(cos_t[:], cos).then_inc(tables_loaded, 16)
            sp.dma_start(sin_t[:], sin).then_inc(tables_loaded, 16)
            sp.wait_ge(stacks_zeroed, 6)
            for i in range(2):
                for par in range(2):
                    sp.dma_start(k_stack[i][64 * par + 48:64 * par + 49, :, :], ones[:]).then_inc(stacks_set, 16)
            sp.wait_ge(stacks_set, 64)

            def read_stack(stack, heads, part, rows):
                for par in range(2):
                    for at, lo in enumerate(rows):
                        img = image[2 * part + lo].rearrange("(j a r) n -> a r j n", a=2, r=DH)[par]
                        sp.dma_start(stack[64 * par + DH * at:64 * par + DH * at + DH, heads(par), :], img).then_inc(
                            k_stacked if part else q_stacked, 16)

            def slot(s, g):
                G = 4 * s.b + g
                if group(G - 1):
                    ps, pg = of_group(s, g, 1)
                    hold(sp, issue, mt_copied, G)
                    for par in range(2):
                        sp.dma_start(q_stack[ps.par][64 * par + 48:64 * par + 49, GH * pg + par:GH * pg + GH:2, :],
                                     mneg[(g - 1) % 2][par:GH:2, :]).then_inc(rows_set[(g - 1) % 2], 16)
                if g == 0 and sample(s + -2):
                    n = s + -2
                    hold(sp, issue, res_done, 2 * n.b + 2)
                    sp.dma_start(dst_v[bass.ds(n.b, 1)].rearrange("b p t d -> p (b t) d"),
                                 res[n.par][:]).then_inc(stored[n.par], 16)
                if g == 0 and sample(s + -1):
                    n = s + -1
                    hold(sp, issue, stored[n.par], 16 * n.half)
                    sp.dma_start(res[n.par][:],
                                 src_v[bass.ds(n.b, 1)].rearrange("b p t d -> p (b t) d")).then_inc(res_loaded[n.par], 16)
                if g == (1 if not isinstance(s.b, int) or s.b > -2 else 2) and sample(s + 2):
                    n = s + 2
                    hold(sp, issue, xn_done, NT * n.b)
                    sp.dma_start(x[:], src_v[bass.ds(n.b, 1)].rearrange("b p t d -> p (b t) d")).then_inc(x_loaded, 16)
                if g == 1 and sample(s + 1):
                    n = s + 1
                    hold(sp, issue, qk_lo, 4 * n.b + 2)
                    for part, t in ((0, qk.hi), (1, qk.lo)):
                        sp.dma_start(image[part].rearrange("(c p) n -> p c n", p=P), t[:, 0:2, :]).then_inc(q_written, 16)
                if g == 2 and sample(s + 1):
                    n = s + 1
                    hold(sp, issue, st_done, 40 * (n.b - 1))
                    hold(sp, issue, q_written, 32 * (n.b + 1))
                    read_stack(q_stack[n.par], lambda par: slice(par, H, 2), 0, (0, 0, 1))
                    for par in range(2):
                        sp.dma_start(q_stack[n.par][64 * par + 48:64 * par + 49, par::2, :], zeros[:]).then_inc(q_stacked, 16)
                    hold(sp, issue, qk_lo, 4 * n.b + 4)
                    for part, t in ((2, qk.hi), (3, qk.lo)):
                        sp.dma_start(image[part].rearrange("(c p) n -> p c n", p=P), t[:, 2:4, :]).then_inc(k_written, 16)
                if g == 3 and sample(s + 1):
                    n = s + 1
                    hold(sp, issue, k_written, 32 * (n.b + 1))
                    read_stack(k_stack[n.par], lambda par: slice(0, H // 2), 1, (0, 1, 0))
                    hold(sp, issue, k_stacked, 96 * (n.b + 1))
                    hold(sp, issue, q_stacked, 128 * (n.b + 1))

            schedule(sp, slot)
            for i in range(2):
                hold(sp, issue, stored[i], 16 * (B // 2))

        @block.gpsimd
        def _(pool):
            for i in range(2):
                nc.gpsimd.memset(q_stack[i][:], 0.0).then_inc(stacks_zeroed, 1)
                nc.gpsimd.memset(k_stack[i][:], 0.0).then_inc(stacks_zeroed, 1)
            nc.gpsimd.memset(ones[:], 1.0).then_inc(stacks_zeroed, 1)
            nc.gpsimd.memset(zeros[:], 0.0).then_inc(stacks_zeroed, 1)

            def mask(G, at, ap, dims):
                pool.sem_inc(mask_starts, 1)
                nc.gpsimd.affine_select(out=ap, in_=ap, compare_op=ALU.is_ge, fill=0.0, base=0,
                                        pattern=[[0, d] for d in dims] + [[1, P]], channel_multiplier=-1).then_inc(masked, 1)

            def rope(n, t):
                idx = 4 * n.b + t
                pool.wait_ge(rope_in, idx + 1)
                nc.gpsimd.tensor_tensor(by_sin[t % 2][:], swapped[t % 2][:], sin_t[:], ALU.mult).then_inc(sin_done, 1)
                wait(pool, qk_lo, idx - 1)
                pool.wait_ge(sin_done, idx + 1)
                nc.gpsimd.tensor_tensor(rotated[t % 2][:], by_cos[t % 2][:], by_sin[t % 2][:], ALU.add).then_inc(rope_done, 1)

            pool.wait_ge(tables_loaded, 32)

            def slot(s, g):
                G = 4 * s.b + g
                if group(G - 2):
                    pool.wait_ge(exp_done, 10 * (G - 2) + 4)
                    mask(G, 0, probs[:, 0:4, 0:P], (4,))
                if g < 2 and sample(s + 1):
                    rope(s + 1, 2 * g)
                if group(G - 2):
                    pool.wait_ge(exp_done, 10 * (G - 2) + 8)
                    mask(G, 1, probs[:, 4:8, 0:P], (4,))
                    mask(G, 2, probs[:, 4:8, 3 * P:4 * P], (4,))
                    pool.wait_ge(exp_done, 10 * (G - 2) + 10)
                    mask(G, 3, probs[:, 8:10, :].rearrange("p c (a n) -> p (c a) n", a=2)[:, :, 0:P], (4,))
                if g < 2 and sample(s + 1):
                    rope(s + 1, 2 * g + 1)
                if g == 2 and sample(s + 2):
                    n = s + 2
                    pool.wait_ge(stats_done, n.b + 1)
                    nc.gpsimd.tensor_tensor(rstd[:], ve[:, 0, :], tab.minus_half[:, 0:NT], ALU.pow).then_inc(rstd_done, 1)
                    wait(pool, xT_done, NC * n.b)
                    pool.wait_ge(rstd_done, n.b + 1)
                    pool.sem_inc(xn_starts, 1)
                    for t in range(NT):
                        nc.gpsimd.tensor_scalar(xn[:, t, :], x[:, t, :], ve[:, 1, t:t + 1], rstd[:, t:t + 1],
                                                ALU.add, ALU.mult).then_inc(xn_done, 1)

            schedule(pool, slot)

        @block.vector
        def _(dve):
            for i in range(2):
                nc.vector.memset(v[i][:], 1.0).then_inc(consts_set, 1)

            def begin_rope(n, t):
                idx = 4 * n.b + t
                dve.wait_ge(qk_done, idx + 1)
                wait(dve, rope_done, idx - 1)
                nc.vector.tensor_tensor(by_cos[t % 2][:], x_ps[t % 2][:], cos_t[:], ALU.mult)
                nc.vector.stream_shuffle(swapped[t % 2][:], x_ps[t % 2][:], [i ^ 1 for i in range(32)]).then_inc(rope_in, 1)

            def rope_low(n, t):
                dve.wait_ge(qk_hi, 4 * n.b + t + 1)
                wait(dve, q_written if t < 2 else k_written, 32 * n.b)
                nc.vector.tensor_tensor(qk.lo[:, t, :], rotated[t % 2][:], qk.hi[:, t, :], ALU.subtract).then_inc(qk_lo, 1)

            def maxima(s, g, n):
                G = 4 * s.b + g
                dve.wait_ge(mx_done, 11 * G + n + 1)
                if n == 0:
                    wait(dve, mt_done, G - 1)
                bank = mx_ps[(n + 1) % 2]
                out = mx[g % 2]
                if n < 4:
                    i, o_ap, i_ap = 3, out[:, 3, n:n + 1], bank[:]
                elif n < 8:
                    o_ap, i_ap = out[:, 2, n - 4:n - 3], bank[:, 0:3 * P]
                elif n < 10:
                    a = 2 * (n - 8)
                    o_ap, i_ap = out[:, 1, a:a + 2], bank[:].rearrange("p (a n) -> p a n", a=2)
                else:
                    o_ap, i_ap = out[:, 0, :], bank[:].rearrange("p (a n) -> p a n", a=4)
                nc.vector.tensor_reduce(o_ap, i_ap, AX_X, ALU.max).then_inc(max_done, 1)

            dve.wait_ge(tables_loaded, 32)
            dve.wait_ge(consts_set, 2)

            def slot(s, g):
                G = 4 * s.b + g
                cur = group(G)
                if cur:
                    for n in range(0, 3):
                        maxima(s, g, n)
                if group(G - 3):
                    os, og = of_group(s, g, 3)
                    turned = pv_ps[:].rearrange("p (i a d) -> p i a d", i=NT, a=GH)
                    dve.wait_ge(o_turned, G - 2)
                    nc.vector.reciprocal(inverse[:].rearrange("p (i a) -> p i a", i=NT), turned[:, :, :, DH]).then_inc(inverse_done, 1)
                    wait(dve, oT_done, NC * (os.b - 1))
                    dve.wait_ge(inverse_done, G - 2)
                    for i in range(NT):
                        ins = nc.vector.tensor_tensor(
                            on[os.par][:, i, GH * DH * og:GH * DH * (og + 1)].rearrange("p (a d) -> p a d", a=GH),
                            turned[:, i, :, 0:DH],
                            inverse[:, GH * i:GH * i + GH].rearrange("p (a d) -> p a d", d=1).broadcast_to([P, GH, DH]), ALU.mult)
                    ins.then_inc(on_done, 1)
                if cur:
                    maxima(s, g, 3)
                if g in (1, 2) and sample(s + 1):
                    rope_low(s + 1, 2 * (g - 1))
                    rope_low(s + 1, 2 * (g - 1) + 1)
                if g < 2 and sample(s + 1):
                    begin_rope(s + 1, 2 * g)
                if g == 3 and sample(s + 2):
                    n = s + 2
                    for c in range(NC):
                        dve.wait_ge(xT_hi, NC * n.b + c + 1)
                        nc.vector.tensor_tensor(xT.lo[:, c, :], x_ps[c][:], xT.hi[:, c, :], ALU.subtract).then_inc(xT_lo, 1)
                if cur:
                    for n in range(4, 8):
                        maxima(s, g, n)
                if g < 2 and sample(s + 1):
                    begin_rope(s + 1, 2 * g + 1)
                if cur:
                    maxima(s, g, 8)
                if g == 3 and sample(s + -1):
                    n = s + -1
                    for c in range(NC):
                        dve.wait_ge(oT_hi, NC * n.b + c + 1)
                        nc.vector.tensor_tensor(oT.lo[:, c, :], x_ps[c][:], oT.hi[:, c, :], ALU.subtract).then_inc(oT_lo, 1)
                if cur:
                    for n in range(9, 11):
                        maxima(s, g, n)
                if g == 2 and sample(s + 2):
                    n = s + 2
                    dve.wait_ge(x_loaded, 16 * (n.b + 1))
                    wait(dve, xn_done, NT * n.b)
                    layernorm_stats(nc, dve, stats_step, stats_done, n.b, x, stats, pair, ve)
                if g == 3 and sample(s + -1):
                    n = s + -1
                    dve.wait_ge(res_loaded[n.par], 16 * (n.half + 1))
                    for j in range(2):
                        dve.wait_ge(o_done, 2 * n.b + j + 1)
                        r = res[n.par][:, 2 * j:2 * j + 2, :]
                        nc.vector.tensor_tensor(r, x_ps[j][:].rearrange("p (t d) -> p t d", t=2), r, ALU.add).then_inc(res_done, 1)

            schedule(dve, slot)

        @block.scalar
        def _(act):
            def exps(G, cs):
                for c in cs:
                    wait(act, pv_done, 4 * (G - 3) + (1 if c < 4 else 3 if c < 8 else 4))
                    act.wait_ge(st_done, 10 * (G - 2) + c + 1)
                    nc.scalar.activation(probs[:, c, :], st_ps[ST_BANK[c]][:], ACT.Exp, scale=DH ** -0.5).then_inc(exp_done, 1)

            def rope_high(n, t):
                act.wait_ge(rope_done, 4 * n.b + t + 1)
                wait(act, q_written if t < 2 else k_written, 32 * n.b)
                nc.scalar.activation(qk.hi[:, t, :], rotated[t % 2][:], ACT.Copy).then_inc(qk_hi, 1)

            act.wait_ge(consts_set, 2)

            def slot(s, g):
                G = 4 * s.b + g
                if group(G - 1):
                    act.wait_ge(mt_done, G)
                    wait(act, rows_set[(g - 3) % 2], 32 * (2 * s.b + (g - 3) // 2 + 1))
                    nc.scalar.activation(mneg[(g - 1) % 2][:], mx_ps[0][0:GH, :], ACT.Copy, scale=-1.0).then_inc(mt_copied, 1)
                if group(G - 3):
                    act.wait_ge(pv_done, 4 * (G - 2))
                    wait(act, o_turned, G - 3)
                    nc.scalar.activation(o32[:], pv_ps[:], ACT.Copy).then_inc(o_copied, 1)
                run = group(G - 2)
                if run:
                    exps(G, range(0, 2))
                if g in (1, 2) and sample(s + 1):
                    rope_high(s + 1, 2 * (g - 1))
                if run:
                    exps(G, range(2, 4))
                if g in (1, 2) and sample(s + 1):
                    rope_high(s + 1, 2 * (g - 1) + 1)
                if g == 3 and sample(s + 2):
                    n = s + 2
                    wait(act, v_done, 2 * n.b)
                    for c in range(NC):
                        act.wait_ge(xT_done, NC * n.b + c + 1)
                        nc.scalar.activation(xT.hi[:, c, :], x_ps[c][:], ACT.Copy).then_inc(xT_hi, 1)
                if run:
                    exps(G, range(4, 7))
                if g == 2 and sample(s + 1):
                    v_copy(s + 1, 0)
                if run:
                    exps(G, range(7, 9))
                if g == 3 and sample(s + -1):
                    n = s + -1
                    wait(act, o_done, 2 * n.b)
                    for c in range(NC):
                        act.wait_ge(oT_done, NC * n.b + c + 1)
                        nc.scalar.activation(oT.hi[:, c, :], x_ps[c][:], ACT.Copy).then_inc(oT_hi, 1)
                if run:
                    exps(G, range(9, 10))
                if g == 2 and sample(s + 1):
                    v_copy(s + 1, 1)

            def v_copy(n, j):
                act.wait_ge(v_done, 2 * n.b + j + 1)
                wait(act, pv_done, 16 * (n.b - 1))
                for t in range(2):
                    ins = nc.scalar.activation(v[n.par][:, 2 * j + t, :, 0:DH],
                                               x_ps[j][:, t * D:(t + 1) * D].rearrange("p (h d) -> p h d", h=H), ACT.Copy)
                ins.then_inc(v_copied, 1)

            schedule(act, slot)

        @block.tensor
        def _(pe):
            def part(t, p):
                return t.hi if p == "hi" else t.lo

            def turn_maxima(s, g):
                G = 4 * s.b + g
                pe.wait_ge(max_done, 11 * G)
                for i in range(NT):
                    ins = nc.tensor.transpose(mx_ps[0][0:GH, i * P:(i + 1) * P], mx[(g - 1) % 2][:, i, :], tab.ident[:])
                ins.then_inc(mt_done, 1)

            def max_scores(s, g, n):
                G = 4 * s.b + g
                wait(pe, max_done, 11 * G + n - 1 if n > 1 else 11 * G)
                if n == 1:
                    wait(pe, mt_copied, G)
                if n == 0:
                    pe.wait_ge(q_stacked, 128 * (s.b + 1))
                    pe.wait_ge(k_stacked, 96 * (s.b + 1))
                bank = mx_ps[(n + 1) % 2]
                i, heads = (3, [n]) if n < 4 else (2, [n - 4]) if n < 8 else (1, [2 * n - 16, 2 * n - 15]) if n < 10 else (0, range(4))
                w = (i + 1) * P
                for at, a in enumerate(heads):
                    h = GH * g + a
                    nc.tensor.matmul(bank[:, at * w:at * w + w], q_stack[s.par][:, h, i * P:(i + 1) * P],
                                     k_stack[s.par][:, h // 2, 0:w], start=True, stop=False)
                    ins = nc.tensor.matmul(bank[:, at * w + i * P:at * w + w], tab.identb[:], tab.mask[:], start=False, stop=True)
                ins.then_inc(mx_done, 1)

            def scores(s, g, c):
                G = 4 * s.b + g - 2
                ss, sg = of_group(s, g, 2)
                bank = st_ps[ST_BANK[c]]
                before = [x for x in range(c) if ST_BANK[x] == ST_BANK[c]]
                last = before[-1] if before else max(x for x in range(10) if ST_BANK[x] == ST_BANK[c]) - 10
                wait(pe, exp_done, 10 * G + last + 1)
                if c == 0:
                    pe.wait_ge(rows_set[g % 2], 32 * (2 * s.b + (g - 2) // 2 + 1))
                h = GH * sg + (c % 4 if c < 8 else 2 * (c - 8))
                work = [(h, 0, 0, 0)] if c < 4 else [(h, 1, P, 0), (h, 3, 3 * P, 3 * P)] if c < 8 else \
                    [(h, 2, 2 * P, 0), (h + 1, 2, 2 * P, 2 * P)]
                for hh, kt, q0, col in work:
                    ins = nc.tensor.matmul(bank[:, col:col + T - q0], k_stack[ss.par][:, hh // 2, kt * P:(kt + 1) * P],
                                           q_stack[ss.par][:, hh, q0:T], start=True, stop=True)
                ins.then_inc(st_done, 1)

            def probs_v(s, g, nth, kt):
                G = 4 * s.b + g - 2
                ss, sg = of_group(s, g, 2)
                if kt == 0:
                    wait(pe, on_done, G)
                    pe.wait_ge(v_copied, 2 * (ss.b + 1))
                pe.wait_ge(exp_done, 10 * G + (4, 8, 10, 8)[kt])
                pe.wait_ge(masked, 4 * G + nth + 1)
                for a in range(GH):
                    p = (probs[:, a, :], probs[:, 4 + a, 0:3 * P], probs[:, 8 + a // 2, (a % 2) * 2 * P:(a % 2) * 2 * P + 2 * P],
                         probs[:, 4 + a, 3 * P:])[kt]
                    ins = nc.tensor.matmul(pv_ps[32 * a:32 * a + 32, kt * P:T], v[ss.par][:, kt, GH * sg + a, :], p,
                                           start=(kt == 0), stop=(nth == 3), tile_position=(0, 32 * a))
                ins.then_inc(pv_done, 1)

            def project_qk(n, t):
                idx = 4 * n.b + t
                if t == 0:
                    pe.wait_ge(xT_lo, NC * (n.b + 1))
                    wait(pe, res_done, 2 * (n.b - 2))
                if t >= 2:
                    pe.wait_ge(rope_in, idx - 1)
                i = 0
                for c in range(NC):
                    for wp, xp in TERMS:
                        ins = nc.tensor.matmul(x_ps[t % 2][:], part(tab.qkv, wp)[:, c, t * P:(t + 1) * P], part(xT, xp)[:, c, :],
                                               start=(i == 0), stop=(i == 3 * NC - 1))
                        i += 1
                ins.then_inc(qk_done, 1)

            def project_v(n, j):
                pe.wait_ge(rope_in, 4 * (n.b + 1) - 1 + j)
                for t in range(2):
                    i = 0
                    for c in range(NC):
                        for xp, wp in TERMS:
                            ins = nc.tensor.matmul(x_ps[j][:, t * D:(t + 1) * D],
                                                   part(xT, xp)[:, c, (2 * j + t) * P:(2 * j + t + 1) * P],
                                                   part(tab.qkv, wp)[:, c, 2 * D:3 * D], start=(i == 0), stop=(i == 3 * NC - 1))
                            i += 1
                ins.then_inc(v_done, 1)

            def transposes(n):
                pe.wait_ge(xn_done, NT * (n.b + 1))
                wait(pe, v_copied, 2 * n.b)
                for c in range(NC):
                    for t in range(NT):
                        ins = nc.tensor.transpose(x_ps[c][:, t * P:(t + 1) * P], xn[:, t, c * P:(c + 1) * P], tab.ident[:])
                    ins.then_inc(xT_done, 1)

            def turn_output(s, g):
                G = 4 * s.b + g
                pe.wait_ge(o_copied, G - 2)
                for i in range(NT):
                    ins = nc.tensor.transpose(pv_ps[:, i * P:(i + 1) * P], o32[:, i * P:(i + 1) * P], tab.ident[:])
                ins.then_inc(o_turned, 1)

            def transpose_o(n, s):
                pe.wait_ge(on_done, 4 * (n.b + 1))
                if sample(s + 2):
                    pe.wait_ge(xT_lo, NC * (s.b + 3))
                elif sample(s + 1):
                    pe.wait_ge(v_copied, 2 * (s.b + 2))
                else:
                    wait(pe, res_done, 2 * n.b)
                for c in range(NC):
                    for i in range(NT):
                        ins = nc.tensor.transpose(x_ps[c][:, i * P:(i + 1) * P], on[n.par][:, i, c * P:(c + 1) * P], tab.ident[:])
                    ins.then_inc(oT_done, 1)

            def project_o(n):
                pe.wait_ge(oT_lo, NC * (n.b + 1))
                for t in range(NT):
                    i = 0
                    for c in range(NC):
                        for op, wp in TERMS:
                            ins = nc.tensor.matmul(x_ps[t // 2][:, (t % 2) * D:(t % 2) * D + D], part(oT, op)[:, c, t * P:(t + 1) * P],
                                                   part(tab.wo, wp)[:, c, :], start=(i == 0), stop=(i == 3 * NC - 1))
                            i += 1
                    if t % 2:
                        ins.then_inc(o_done, 1)

            def slot(s, g):
                G = 4 * s.b + g
                cur, run = group(G), group(G - 2)

                def pairs(lo, hi):
                    for n in range(lo, hi):
                        if run and n < 10:
                            scores(s, g, n)
                        if cur:
                            max_scores(s, g, n)

                if group(G - 1):
                    turn_maxima(s, g)
                pairs(0, 3)
                if group(G - 3):
                    turn_output(s, g)
                pairs(3, 4)
                if g < 2 and sample(s + 1):
                    project_qk(s + 1, 2 * g)
                if g == 2 and sample(s + 1):
                    project_v(s + 1, 0)
                if g == 3 and sample(s + 2):
                    transposes(s + 2)
                pairs(4, 6)
                if run:
                    probs_v(s, g, 0, 0)
                pairs(6, 8)
                if g < 2 and sample(s + 1):
                    project_qk(s + 1, 2 * g + 1)
                if g == 3 and sample(s + -1):
                    transpose_o(s + -1, s)
                pairs(8, 11)
                if run:
                    probs_v(s, g, 1, 1)
                    probs_v(s, g, 2, 3)
                if g == 2 and sample(s + 1):
                    project_v(s + 1, 1)
                if run:
                    probs_v(s, g, 3, 2)
                if g == 3 and sample(s + -1):
                    project_o(s + -1)

            pe.wait_ge(stacks_set, 64)
            schedule(pe, slot)


def program(nc, x, WqkvT, WoT, Wr, br, W1, b1T, W2, b2, cos, sin, out):
    with ExitStack() as ctx:
        sb = lambda n, s, d: ctx.enter_context(nc.sbuf_tensor(n, s, d))
        tab = Tables()
        tab.w1 = Split(sb("w1_hi", [P, E, NC * D], F16), sb("w1_lo", [P, E, NC * D], F16))
        tab.w2 = Split(sb("w2_hi", [P, E, NC * D], F16), sb("w2_lo", [P, E, NC * D], F16))
        tab.b1 = sb("b1_table", [P, E, NC], F32)
        tab.qkv = Split(sb("qkv_hi", [P, NC, 3 * D], F16), sb("qkv_lo", [P, NC, 3 * D], F16))
        tab.wo = Split(sb("wo_hi", [P, NC, D], F16), sb("wo_lo", [P, NC, D], F16))
        tab.ident = sb("ident", [P, P], F32)
        tab.identb = sb("identb", [P, P], BF16)
        tab.mask = sb("mask", [P, P], BF16)
        tab.quarter = sb("quarter", [P, D], F32)
        tab.minus_half = sb("minus_half", [P, NT], F32)
        build_tables(nc, tab, W1, W2, b1T, WqkvT, WoT)
        x1 = nc.dram_tensor("after_ffn1", (B, T, D), F32, kind="Internal").ap()
        x2 = nc.dram_tensor("after_attention", (B, T, D), F32, kind="Internal").ap()
        ffn_phase(nc, "f1", tab, x, x1, Wr, br, b2)
        attention_phase(nc, tab, x1, x2, cos, sin)
        ffn_phase(nc, "f2", tab, x2, out, Wr, br, b2)


_OUT = ((B, T, D), "float32")


def kernel(L0_attn_x, L0_attn_Wqkv, L0_attn_Wo, L0_ffn_Wr, L0_ffn_br, L0_ffn_W1, L0_ffn_b1, L0_ffn_W2, L0_ffn_b2):
    import numpy as np
    import concourse.bacc as bacc
    from concourse.bass_utils import run_bass_kernel_spmd

    freqs = np.exp(np.float32(-np.log(10000.0)) * np.arange(0, DH, 2, dtype=np.float32) / np.float32(DH)).astype(np.float32)
    angles = np.arange(T, dtype=np.float32)[None, :] * freqs[(np.arange(P) % DH) // 2][:, None]
    sign = np.where(np.arange(P) % 2 == 0, -1.0, 1.0).astype(np.float32)[:, None]
    ins = {
        "x": L0_attn_x,
        "WqkvT": np.asarray(L0_attn_Wqkv).T,
        "WoT": np.asarray(L0_attn_Wo).T,
        "Wr": L0_ffn_Wr,
        "br": L0_ffn_br,
        "W1": L0_ffn_W1,
        "b1T": np.asarray(L0_ffn_b1).reshape(E, NC, P).transpose(2, 0, 1),
        "W2": L0_ffn_W2,
        "b2": L0_ffn_b2,
        "cos": np.cos(angles).astype(np.float32),
        "sin": (np.sin(angles) * sign).astype(np.float32),
    }
    nc = bacc.Bacc("TRN2", target_bir_lowering=False, num_devices=1)
    arrays, args = {}, []
    for name, a in ins.items():
        a = np.ascontiguousarray(a)
        arrays[f"in_{name}"] = a
        args.append(nc.dram_tensor(f"in_{name}", a.shape, mybir.dt.from_np(a.dtype), kind="ExternalInput").ap())
    args.append(nc.dram_tensor("out_0", _OUT[0], mybir.dt.from_np(np.dtype(_OUT[1])), kind="ExternalOutput").ap())
    program(nc, *args)
    r = run_bass_kernel_spmd(nc, [arrays], core_ids=[0])
    return r.results[0]["out_0"]
```

```python
from contextlib import ExitStack

import concourse.bass as bass
from concourse import mybir

ALU = mybir.AluOpType
ACT = mybir.ActivationFunctionType
AX_X = mybir.AxisListType.X
F32 = mybir.dt.float32
F16 = mybir.dt.float16
BF16 = mybir.dt.bfloat16
I32 = mybir.dt.int32
U32 = mybir.dt.uint32

P = 128
B, T, D = 32, 512, 256
E, TOP_K = 8, 2
NT = T // P
NC = D // P
EPS = 1e-5
H = 16
DH = D // H
GH = 4
MX_BANK = (0, 1, 0, 1, 2, 0, 1, 2, 0, 1, 2)
TURN_BANK = 2
FIRST_SLOT = -6
HALF = 0.5


class At:

    def __init__(self, k, c):
        self.k, self.c = k, c

    def __add__(self, n):
        return At(self.k, self.c + n)

    @property
    def par(self):
        return self.c % 2

    @property
    def half(self):
        return self.k + self.c // 2

    @property
    def b(self):
        return self.k * 2 + self.c


def wait(eng, sem, value):
    if isinstance(value, int) and value <= 0:
        return
    eng.wait_ge(sem, value)


def hold(sp, issue, sem, value):
    if isinstance(value, int) and value <= 0:
        return
    sp.wait_ge(sem, value)
    sp.sem_inc(issue, 1)


class Tables:
    pass


class Split:

    def __init__(self, hi, lo):
        self.hi, self.lo = hi, lo


TERMS = (("hi", "hi"), ("lo", "hi"), ("hi", "lo"))


def over_samples(eng, step):
    step(At(0, 0), first=True, last=False)
    step(At(0, 1), first=False, last=False)
    with eng.Fori(0, (B - 4) // 2) as k:
        step(At(k, 2), first=False, last=False)
        step(At(k, 3), first=False, last=False)
    step(At(0, B - 2), first=False, last=False)
    step(At(0, B - 1), first=False, last=True)


def layernorm_stats(nc, dve, stats_step, stats_done, b, x, stats, pair, ve):
    for t in range(NT):
        ins = nc.vector.bn_stats(stats[:, t, :], x[:, t, :])
    ins.then_inc(stats_step, 1)
    dve.wait_ge(stats_step, 3 * b + 1)
    nc.vector.tensor_tensor(pair[:, 0, :], stats[:, :, 1], stats[:, :, 4], ALU.add)
    nc.vector.tensor_tensor(pair[:, 1, :], stats[:, :, 1], stats[:, :, 4], ALU.subtract)
    nc.vector.tensor_tensor(pair[:, 2, :], stats[:, :, 2], stats[:, :, 5], ALU.add).then_inc(stats_step, 1)
    dve.wait_ge(stats_step, 3 * b + 2)
    nc.vector.tensor_scalar(ve[:, 1, :], pair[:, 0, :], -0.5, None, ALU.mult)
    nc.vector.tensor_tensor(pair[:, 3, :], pair[:, 1, :], pair[:, 1, :], ALU.mult)
    nc.vector.tensor_scalar(pair[:, 4, :], pair[:, 2, :], 1.0 / D, EPS, ALU.mult, ALU.add).then_inc(stats_step, 1)
    dve.wait_ge(stats_step, 3 * b + 3)
    nc.vector.scalar_tensor_tensor(out=ve[:, 0, :], in0=pair[:, 3, :], scalar=0.25, in1=pair[:, 4, :],
                                   op0=ALU.mult, op1=ALU.add).then_inc(stats_done, 1)


def build_tables(nc, tab, W1, W2, b1T, WqkvT, WoT):
    with ExitStack() as ctx:
        sb = lambda n, s, d: ctx.enter_context(nc.sbuf_tensor(n, s, d))
        sem = lambda n: ctx.enter_context(nc.semaphore(n))
        w1f = sb("w1_stage", [P, E, NC * D], F32)
        w2f = sb("w2_stage", [P, E, NC * D], F32)
        qkvf = sb("qkv_stage", [P, NC, 3 * D], F32)
        wof = sb("wo_stage", [P, NC, D], F32)
        loaded = {n: sem(f"{n}_loaded") for n in ("w1", "w2", "b1", "qkv", "wo")}
        ident_zeroed = sem("ident_zeroed")
        w1_hi, w2_hi, small_hi, tables_done = sem("w1_hi"), sem("w2_hi"), sem("small_hi"), sem("tables_done")
        block = ctx.enter_context(nc.Block())

        @block.sync
        def _(sp):
            sp.dma_start(w1f[:].rearrange("p e (c n) -> p e c n", c=NC),
                         W1.rearrange("e (c p) n -> p e c n", p=P)).then_inc(loaded["w1"], 16)
            sp.dma_start(w2f[:].rearrange("p e (c n) -> p e c n", c=NC),
                         W2.rearrange("e (c p) n -> p e c n", p=P)).then_inc(loaded["w2"], 16)
            sp.dma_start(tab.b1[:], b1T).then_inc(loaded["b1"], 16)
            sp.wait_ge(loaded["b1"], 16)

        @block.scalar
        def _(act):
            act.dma_start(qkvf[:], WqkvT.rearrange("(c p) n -> p c n", p=P)).then_inc(loaded["qkv"], 16)
            act.dma_start(wof[:], WoT.rearrange("(c p) n -> p c n", p=P)).then_inc(loaded["wo"], 16)
            act.wait_ge(loaded["w1"], 16)
            nc.scalar.activation(tab.w1.hi[:], w1f[:], ACT.Copy).then_inc(w1_hi, 1)
            act.wait_ge(loaded["qkv"], 16)
            nc.scalar.activation(tab.qkv.hi[:], qkvf[:], ACT.Copy).then_inc(small_hi, 1)
            act.wait_ge(loaded["wo"], 16)
            nc.scalar.activation(tab.wo.hi[:], wof[:], ACT.Copy).then_inc(small_hi, 1)

        @block.vector
        def _(dve):
            dve.wait_ge(loaded["w2"], 16)
            nc.vector.tensor_copy(tab.w2.hi[:], w2f[:]).then_inc(w2_hi, 1)
            dve.wait_ge(w1_hi, 1)
            nc.vector.tensor_tensor(tab.w1.lo[:], w1f[:], tab.w1.hi[:], ALU.subtract).then_inc(tables_done, 1)
            dve.wait_ge(w2_hi, 1)
            nc.vector.tensor_tensor(tab.w2.lo[:], w2f[:], tab.w2.hi[:], ALU.subtract).then_inc(tables_done, 1)
            dve.wait_ge(small_hi, 2)
            nc.vector.tensor_tensor(tab.qkv.lo[:], qkvf[:], tab.qkv.hi[:], ALU.subtract).then_inc(tables_done, 1)
            nc.vector.tensor_tensor(tab.wo.lo[:], wof[:], tab.wo.hi[:], ALU.subtract).then_inc(tables_done, 1)
            dve.wait_ge(tables_done, 8)

        @block.gpsimd
        def _(pool):
            nc.gpsimd.memset(tab.ident[:], 0.0).then_inc(ident_zeroed, 1)
            nc.gpsimd.memset(tab.minus_half[:], -0.5).then_inc(tables_done, 1)
            nc.gpsimd.memset(tab.quarter[:], HALF / TOP_K).then_inc(tables_done, 1)
            nc.gpsimd.memset(tab.identb[:], 0.0).then_inc(ident_zeroed, 1)
            nc.gpsimd.memset(tab.mask[:], 0.0).then_inc(ident_zeroed, 1)
            pool.wait_ge(ident_zeroed, 3)
            nc.gpsimd.affine_select(out=tab.ident[:], in_=tab.ident[:], compare_op=ALU.not_equal, fill=1.0,
                                    base=0, pattern=[[-1, P]], channel_multiplier=1).then_inc(tables_done, 1)
            nc.gpsimd.affine_select(out=tab.identb[:], in_=tab.identb[:], compare_op=ALU.not_equal, fill=1.0,
                                    base=0, pattern=[[-1, P]], channel_multiplier=1).then_inc(ident_zeroed, 1)
            nc.gpsimd.affine_select(out=tab.mask[:], in_=tab.mask[:], compare_op=ALU.is_ge, fill=-1e30,
                                    base=0, pattern=[[-1, P]], channel_multiplier=1).then_inc(tables_done, 1)
            pool.wait_ge(ident_zeroed, 4)


def ffn_phase(nc, tag, tab, src, dst, Wr, br, b2):
    with ExitStack() as ctx:
        sb = lambda n, s, d: ctx.enter_context(nc.sbuf_tensor(f"{tag}_{n}", s, d))
        pb = lambda n, s, d: ctx.enter_context(nc.psum_tensor(f"{tag}_{n}", s, d))
        sem = lambda n: ctx.enter_context(nc.semaphore(f"{tag}_{n}"))

        row = sb("row", [B, D], F32)
        row_n = sb("row_n", [B, D], F32)
        row_stats = sb("row_stats", [B, 6], F32)
        row_mv = sb("row_mv", [B, 2], F32)
        row_ve = sb("row_ve", [B, 2], F32)
        row_rstd = sb("row_rstd", [B, 1], F32)
        rowT = sb("rowT", [P, NC, B], F32)
        wr = sb("wr", [P, NC, E], F32)
        brb = sb("brb", [B, E], F32)
        logits = sb("logits", [B, E], F32)
        top = sb("top", [B, 8], F32)
        top_i = sb("top_i", [B, 8], U32)
        routes = sb("routes", [1, B * TOP_K], U32)
        x = [sb(f"x{i}", [P, NT, D], F32) for i in range(2)]
        xn = sb("xn", [P, NT, D], F32)
        stats = sb("stats", [P, NT, 6], F32)
        pair = sb("pair", [P, 5, NT], F32)
        ve = sb("ve", [P, 2, NT], F32)
        rstd = sb("rstd", [P, NT], F32)
        xT = [Split(sb(f"xThi{i}", [P, NC, T], F16), sb(f"xTlo{i}", [P, NC, T], F16)) for i in range(2)]
        w1 = [Split(sb(f"w1hi{i}", [P, TOP_K, NC * D], F16), sb(f"w1lo{i}", [P, TOP_K, NC * D], F16)) for i in range(2)]
        w2 = [Split(sb(f"w2hi{i}", [P, TOP_K, NC * D], F16), sb(f"w2lo{i}", [P, TOP_K, NC * D], F16)) for i in range(2)]
        b1s = [sb(f"b1s{i}", [P, TOP_K, NC], F32) for i in range(2)]
        b2s = [sb(f"b2s{i}", [P, TOP_K, D], F32) for i in range(2)]
        b2sum = sb("b2sum", [P, D], F32)
        b2q = sb("b2q", [P, D], F32)
        h32 = [sb(f"h32_{i}", [P, T], F32) for i in range(4)]
        h = [Split(sb(f"hhi{i}", [P, 4, T], F16), sb(f"hlo{i}", [P, 4, T], F16)) for i in range(2)]
        res = [sb(f"res{i}", [P, NT, D], F32) for i in range(2)]
        xT_ps = [pb(f"xT_ps{c}", [P, T], F32) for c in range(NC)]
        h_ps = [pb(f"h_ps{j}", [P, T], F32) for j in range(4)]
        y_ps = [pb(f"y_ps{j}", [P, 2, D], F32) for j in range(2)]

        row_loaded, wr_loaded, routes_loaded = sem("row_loaded"), sem("wr_loaded"), sem("routes_loaded")
        r_stats, r_rstd, r_norm = sem("r_stats"), sem("r_rstd"), sem("r_norm")
        r_T, r_Tcopied, r_logits, r_top = sem("r_T"), sem("r_Tcopied"), sem("r_logits"), sem("r_top")
        x_loaded = [sem(f"x_loaded{i}") for i in range(2)]
        w1_loaded = [sem(f"w1_loaded{i}") for i in range(2)]
        w2_loaded = [sem(f"w2_loaded{i}") for i in range(2)]
        b2_loaded = [sem(f"b2_loaded{i}") for i in range(2)]
        stored = [sem(f"stored{i}") for i in range(2)]
        norm_starts, issue = sem("norm_starts"), sem("issue")
        stats_step, stats_done, rstd_done, xn_done = sem("stats_step"), sem("stats_done"), sem("rstd_done"), sem("xn_done")
        xT_done, xT_hi, xT_lo = sem("xT_done"), sem("xT_hi"), sem("xT_lo")
        h_done, gelu_done, h_lo, y_done = sem("h_done"), sem("gelu_done"), sem("h_lo"), sem("y_done")
        b2_step, res_ready, out_done = sem("b2_step"), sem("res_ready"), sem("out_done")
        block = ctx.enter_context(nc.Block())

        src_v = src.rearrange("b (p t) d -> b p (t d)", t=NT)
        dst_v = dst.rearrange("b (p t) d -> b p (t d)", t=NT)

        def load_x(sp, s):
            hold(sp, issue, xn_done, NT * s.b - NT)
            hold(sp, issue, res_ready, s.b - 1)
            sp.dma_start(x[s.par][:].rearrange("p t d -> p (t d)"),
                         src_v[bass.ds(s.b, 1)].rearrange("b p n -> p (b n)")).then_inc(x_loaded[s.par], 16)

        def route(sp, s, k):
            return sp.value_load(routes[0:1, bass.ds(s.b * TOP_K + k, 1)], min_val=0, max_val=E - 1)

        @block.sync
        def _(sp):
            sp.dma_start(row[:], src[:, 0, :]).then_inc(row_loaded, 16)
            sp.dma_start(wr[:], Wr.rearrange("(c p) e -> p c e", p=P)).then_inc(wr_loaded, 16)
            sp.dma_start(brb[:], br.rearrange("(a e) -> a e", a=1).broadcast_to([B, E])).then_inc(wr_loaded, 16)
            load_x(sp, At(0, 0))
            load_x(sp, At(0, 1))
            sp.wait_ge(r_top, 2)
            sp.dma_start(routes[:].rearrange("a (b k) -> a b k", k=TOP_K), top_i[:, 0:TOP_K]).then_inc(routes_loaded, 16)
            sp.wait_ge(routes_loaded, 16)

            def load_first(s):
                e = [route(sp, s, k) for k in range(TOP_K)]
                hold(sp, issue, h_done, 4 * s.b - 4)
                hold(sp, issue, gelu_done, 8 * s.b - 8)
                for k in range(TOP_K):
                    sp.dma_start(w1[s.par].hi[:, k, :], tab.w1.hi[:, bass.ds(e[k], 1), :]).then_inc(w1_loaded[s.par], 16)
                    sp.dma_start(w1[s.par].lo[:, k, :], tab.w1.lo[:, bass.ds(e[k], 1), :]).then_inc(w1_loaded[s.par], 16)
                    sp.dma_start(b1s[s.par][:, k, :], tab.b1[:, bass.ds(e[k], 1), :]).then_inc(w1_loaded[s.par], 16)
                hold(sp, issue, res_ready, s.b - 1)
                for k in range(TOP_K):
                    sp.dma_start(b2s[s.par][:, k, :], b2[bass.ds(e[k], 1), :].broadcast_to([P, D])).then_inc(b2_loaded[s.par], 16)
                return e

            def load_second(s, e):
                hold(sp, issue, y_done, 2 * s.b - 2)
                for k in range(TOP_K):
                    sp.dma_start(w2[s.par].hi[:, k, :], tab.w2.hi[:, bass.ds(e[k], 1), :]).then_inc(w2_loaded[s.par], 16)
                    sp.dma_start(w2[s.par].lo[:, k, :], tab.w2.lo[:, bass.ds(e[k], 1), :]).then_inc(w2_loaded[s.par], 16)

            load_second(At(0, 0), load_first(At(0, 0)))

            def step(s, last_x):
                e = load_first(s + 1)
                if not last_x:
                    load_x(sp, s + 2)
                load_second(s + 1, e)
                if not (isinstance(s.b, int) and s.b == 0):
                    store(s + -1)

            def store(s):
                hold(sp, issue, out_done, 2 * s.b + 2)
                sp.dma_start(dst_v[bass.ds(s.b, 1)].rearrange("b p n -> p (b n)"),
                             res[s.par][:].rearrange("p t d -> p (t d)")).then_inc(stored[s.par], 16)

            step(At(0, 0), False)
            step(At(0, 1), False)
            with sp.Fori(0, (B - 4) // 2) as k:
                step(At(k, 2), False)
                step(At(k, 3), False)
            step(At(0, B - 2), True)
            store(At(0, B - 2))
            store(At(0, B - 1))
            for i in range(2):
                hold(sp, issue, stored[i], 16 * (B // 2))

        @block.gpsimd
        def _(pool):
            pool.wait_ge(r_stats, 4)
            nc.gpsimd.tensor_tensor(row_rstd[:], row_ve[:, 0:1], tab.minus_half[0:B, 0:1], ALU.pow).then_inc(r_rstd, 1)
            pool.wait_ge(r_rstd, 1)
            nc.gpsimd.tensor_scalar(row_n[:], row[:], row_ve[:, 1:2], row_rstd[:, 0:1], ALU.add, ALU.mult).then_inc(r_norm, 1)

            def norm(s):
                pool.wait_ge(stats_done, s.b + 1)
                nc.gpsimd.tensor_tensor(rstd[:], ve[:, 0, :], tab.minus_half[:, 0:NT], ALU.pow).then_inc(rstd_done, 1)
                wait(pool, xT_done, NC * s.b)
                pool.wait_ge(rstd_done, s.b + 1)
                pool.sem_inc(norm_starts, 1)
                for t in range(NT):
                    nc.gpsimd.tensor_scalar(xn[:, t, :], x[s.par][:, t, :], ve[:, 1, t:t + 1], rstd[:, t:t + 1],
                                            ALU.add, ALU.mult).then_inc(xn_done, 1)

            def residual(s):
                pool.wait_ge(b2_loaded[s.par], 16 * TOP_K * (s.half + 1))
                pool.wait_ge(x_loaded[s.par], 16 * (s.half + 1))
                wait(pool, stored[s.par], 16 * s.half)
                nc.gpsimd.tensor_tensor(b2sum[:], b2s[s.par][:, 0, :], b2s[s.par][:, 1, :], ALU.add).then_inc(b2_step, 1)
                pool.wait_ge(b2_step, 2 * s.b + 1)
                nc.gpsimd.tensor_tensor(b2q[:], b2sum[:], tab.quarter[:], ALU.mult).then_inc(b2_step, 1)
                pool.wait_ge(b2_step, 2 * s.b + 2)
                nc.gpsimd.tensor_tensor(res[s.par][:], x[s.par][:],
                                        b2q[:].rearrange("p (t d) -> p t d", t=1).broadcast_to([P, NT, D]),
                                        ALU.add).then_inc(res_ready, 1)

            norm(At(0, 0))

            def step(s, first, last):
                if not last:
                    norm(s + 1)
                residual(s)

            over_samples(pool, step)

        @block.vector
        def _(dve):
            dve.wait_ge(row_loaded, 16)
            nc.vector.bn_stats(row_stats[:], row[:]).then_inc(r_stats, 1)
            dve.wait_ge(r_stats, 1)
            nc.vector.bn_aggr(row_mv[:], row_stats[:]).then_inc(r_stats, 1)
            dve.wait_ge(r_stats, 2)
            nc.vector.tensor_scalar(row_ve[:, 0:1], row_mv[:, 1:2], EPS, None, ALU.add).then_inc(r_stats, 1)
            nc.vector.tensor_scalar(row_ve[:, 1:2], row_mv[:, 0:1], -1.0, None, ALU.mult).then_inc(r_stats, 1)
            dve.wait_ge(r_T, 1)
            nc.vector.tensor_copy(rowT[:].rearrange("p c b -> p (c b)"), xT_ps[0][:, 0:NC * B]).then_inc(r_Tcopied, 1)
            dve.wait_ge(r_logits, 1)
            dve.wait_ge(wr_loaded, 32)
            nc.vector.tensor_tensor(logits[:], xT_ps[1][0:B, 0:E], brb[:], ALU.add).then_inc(r_Tcopied, 1)
            dve.wait_ge(r_Tcopied, 2)
            nc.vector.max(top[:], logits[:]).then_inc(r_top, 1)
            dve.wait_ge(r_top, 1)
            nc.vector.max_index(top_i[:], top[:], logits[:]).then_inc(r_top, 1)

            def norm_stats(s):
                dve.wait_ge(x_loaded[s.par], 16 * (s.half + 1))
                wait(dve, xn_done, NT * s.b)
                layernorm_stats(nc, dve, stats_step, stats_done, s.b, x[s.par], stats, pair, ve)

            def xT_low(s):
                for c in range(NC):
                    dve.wait_ge(xT_hi, NC * s.b + c + 1)
                    nc.vector.tensor_tensor(xT[s.par].lo[:, c, :], xT_ps[c][:], xT[s.par].hi[:, c, :],
                                            ALU.subtract).then_inc(xT_lo, 1)

            norm_stats(At(0, 0))
            xT_low(At(0, 0))
            norm_stats(At(0, 1))

            def step(s, first, last):
                for j in range(4):
                    dve.wait_ge(gelu_done, 8 * s.b + 2 * j + 2)
                    wait(dve, y_done, 2 * s.b - 2)
                    nc.vector.tensor_tensor(h[s.par].lo[:, j, :], h32[j][:], h[s.par].hi[:, j, :],
                                            ALU.subtract).then_inc(h_lo, 1)
                if not last:
                    xT_low(s + 1)
                if not first:
                    output(s + -1)
                if not (isinstance(s.b, int) and s.b + 2 >= B):
                    norm_stats(s + 2)

            def output(s):
                dve.wait_ge(res_ready, s.b + 1)
                for g in range(2):
                    dve.wait_ge(y_done, 2 * s.b + g + 1)
                    r = res[s.par][:, 2 * g:2 * g + 2, :]
                    nc.vector.scalar_tensor_tensor(out=r, in0=y_ps[g][:], scalar=HALF / TOP_K, in1=r,
                                                   op0=ALU.mult, op1=ALU.add).then_inc(out_done, 1)

            over_samples(dve, step)
            output(At(0, B - 1))

        @block.scalar
        def _(act):
            def xT_high(s):
                for c in range(NC):
                    act.wait_ge(xT_done, NC * s.b + c + 1)
                    wait(act, h_done, 4 * s.b - 4)
                    nc.scalar.activation(xT[s.par].hi[:, c, :], xT_ps[c][:], ACT.Copy).then_inc(xT_hi, 1)

            xT_high(At(0, 0))

            def step(s, first, last):
                act.wait_ge(w1_loaded[s.par], 96 * (s.half + 1))
                wait(act, y_done, 2 * s.b - 2)
                for j in range(4):
                    act.wait_ge(h_done, 4 * s.b + j + 1)
                    wait(act, h_lo, 4 * s.b + j - 3)
                    bias = b1s[s.par][:, j // 2, j % 2:j % 2 + 1]
                    nc.scalar.activation(h32[j][:], h_ps[j][:], ACT.Gelu, bias=bias).then_inc(gelu_done, 1)
                    nc.scalar.activation(h[s.par].hi[:, j, :], h_ps[j][:], ACT.Gelu, bias=bias).then_inc(gelu_done, 1)
                if not last:
                    xT_high(s + 1)

            over_samples(act, step)

        @block.tensor
        def _(pe):
            pe.wait_ge(r_norm, 1)
            for c in range(NC):
                ins = nc.tensor.transpose(xT_ps[0][:, c * B:(c + 1) * B], row_n[:, c * P:(c + 1) * P], tab.ident[0:B, 0:B])
            ins.then_inc(r_T, 1)
            pe.wait_ge(r_Tcopied, 1)
            pe.wait_ge(wr_loaded, 32)
            for c in range(NC):
                ins = nc.tensor.matmul(xT_ps[1][0:B, 0:E], rowT[:, c, :], wr[:, c, :], start=(c == 0), stop=(c == NC - 1))
            ins.then_inc(r_logits, 1)
            pe.wait_ge(r_Tcopied, 2)

            def transposes(s):
                pe.wait_ge(xn_done, NT * (s.b + 1))
                wait(pe, xT_lo, NC * s.b)
                for c in range(NC):
                    for t in range(NT):
                        ins = nc.tensor.transpose(xT_ps[c][:, t * P:(t + 1) * P], xn[:, t, c * P:(c + 1) * P], tab.ident[:])
                    ins.then_inc(xT_done, 1)

            def times_w1(s):
                pe.wait_ge(xT_lo, NC * (s.b + 1))
                pe.wait_ge(w1_loaded[s.par], 96 * (s.half + 1))
                for j in range(4):
                    wait(pe, gelu_done, 8 * s.b + 2 * j - 6)
                    n = 0
                    for c in range(NC):
                        for wp, xp in TERMS:
                            w = (w1[s.par].hi if wp == "hi" else w1[s.par].lo)[:, j // 2, c * D + (j % 2) * P:c * D + (j % 2) * P + P]
                            v = (xT[s.par].hi if xp == "hi" else xT[s.par].lo)[:, c, :]
                            ins = nc.tensor.matmul(h_ps[j][:], w, v, start=(n == 0), stop=(n == 3 * NC - 1))
                            n += 1
                    ins.then_inc(h_done, 1)

            def times_w2(s):
                pe.wait_ge(w2_loaded[s.par], 64 * (s.half + 1))
                pe.wait_ge(h_lo, 4 * (s.b + 1))
                for t in range(NT):
                    if t % 2 == 0:
                        wait(pe, out_done, 2 * s.b + t // 2 - 1)
                    n = 0
                    for j in range(4):
                        for hp, wp in TERMS:
                            v = (h[s.par].hi if hp == "hi" else h[s.par].lo)[:, j, t * P:(t + 1) * P]
                            w = (w2[s.par].hi if wp == "hi" else w2[s.par].lo)[:, j // 2, (j % 2) * D:(j % 2) * D + D]
                            ins = nc.tensor.matmul(y_ps[t // 2][:, t % 2, :], v, w, start=(n == 0), stop=(n == 11))
                            n += 1
                    if t % 2:
                        ins.then_inc(y_done, 1)

            transposes(At(0, 0))

            def step(s, first, last):
                times_w1(s)
                if not last:
                    transposes(s + 1)
                if not first:
                    times_w2(s + -1)

            over_samples(pe, step)
            times_w2(At(0, B - 1))


def attention_phase(nc, tab, src, dst, cos, sin):
    with ExitStack() as ctx:
        sb = lambda n, s, d: ctx.enter_context(nc.sbuf_tensor(f"at_{n}", s, d))
        pb = lambda n, s, d: ctx.enter_context(nc.psum_tensor(f"at_{n}", s, d))
        sem = lambda n: ctx.enter_context(nc.semaphore(f"at_{n}"))

        cos_t, sin_t = sb("cos", [P, T], F32), sb("sin", [P, T], F32)
        zeros = sb("zeros", [H // 2, T], F16)
        ones = sb("ones", [H // 2, T], F16)
        x = sb("x", [P, NT, D], F32)
        xn = sb("xn", [P, NT, D], F32)
        stats = sb("stats", [P, NT, 6], F32)
        pair = sb("pair", [P, 5, NT], F32)
        ve = sb("ve", [P, 2, NT], F32)
        rstd = sb("rstd", [P, NT], F32)
        xT = Split(sb("xThi", [P, NC, T], F16), sb("xTlo", [P, NC, T], F16))
        swapped = [sb(f"swapped{i}", [P, T], F32) for i in range(2)]
        by_cos = [sb(f"by_cos{i}", [P, T], F32) for i in range(2)]
        by_sin = [sb(f"by_sin{i}", [P, T], F32) for i in range(2)]
        rotated = [sb(f"rotated{i}", [P, T], F32) for i in range(2)]
        qk = Split(sb("qk_hi", [P, 4, T], F16), sb("qk_lo", [P, 4, T], F16))
        q_stack = [sb(f"q_stack{i}", [P, H, T], F16) for i in range(2)]
        k_stack = [sb(f"k_stack{i}", [P, H // 2, T], F16) for i in range(2)]
        v = [sb(f"v{i}", [P, NT, H, 2 * DH], F32) for i in range(2)]
        mx = [sb(f"mx{i}", [P, GH, NT], F32) for i in range(2)]
        mneg = [sb(f"mneg{i}", [NT * GH, P], F16) for i in range(2)]
        probs = sb("probs", [P, 10, T], F32)
        o32 = sb("o32", [P, T], F32)
        inverse = sb("inverse", [P, NT * GH], F32)
        on = [sb(f"on{i}", [P, NT, D], F32) for i in range(2)]
        oT = Split(sb("oT_hi", [P, NC, T], F16), sb("oT_lo", [P, NC, T], F16))
        res = [sb(f"res{i}", [P, NT, D], F32) for i in range(2)]
        st_ps = [pb(f"st_ps{i}", [P, T], F32) for i in range(2)]
        mx_ps = [pb(f"mx_ps{i}", [P, T], F32) for i in range(3)]
        pv_ps = pb("pv_ps", [P, T], F32)
        x_ps = [pb(f"x_ps{i}", [P, T], F32) for i in range(2)]
        image = nc.dram_tensor("qk_image", (4, D, T), F16, kind="Internal").ap()

        tables_loaded, stacks_zeroed, stacks_set, consts_set = sem("tables_loaded"), sem("stacks_zeroed"), sem("stacks_set"), sem("consts_set")
        x_loaded, q_written, k_written, q_stacked = sem("x_loaded"), sem("q_written"), sem("k_written"), sem("q_stacked")
        k_stacked, stats_step, stats_done, rstd_done = sem("k_stacked"), sem("stats_step"), sem("stats_done"), sem("rstd_done")
        xn_starts, xn_done, xT_done, xT_hi = sem("xn_starts"), sem("xn_done"), sem("xT_done"), sem("xT_hi")
        xT_lo, qk_done, rope_in, sin_done = sem("xT_lo"), sem("qk_done"), sem("rope_in"), sem("sin_done")
        rope_done, qk_hi, qk_lo, v_done = sem("rope_done"), sem("qk_hi"), sem("qk_lo"), sem("v_done")
        v_copied, mx_done, max_done, mt_done = sem("v_copied"), sem("mx_done"), sem("max_done"), sem("mt_done")
        mt_copied, st_done, exp_done, masked = sem("mt_copied"), sem("st_done"), sem("exp_done"), sem("masked")
        pv_done, o_copied, o_turned, inverse_done = sem("pv_done"), sem("o_copied"), sem("o_turned"), sem("inverse_done")
        on_done, oT_done, oT_hi, oT_lo = sem("on_done"), sem("oT_done"), sem("oT_hi"), sem("oT_lo")
        o_done, res_done, issue, mask_starts = sem("o_done"), sem("res_done"), sem("issue"), sem("mask_starts")
        res_loaded = [sem(f"res_loaded{i}") for i in range(2)]
        stored = [sem(f"stored{i}") for i in range(2)]
        rows_set = [sem(f"rows_set{i}") for i in range(2)]
        block = ctx.enter_context(nc.Block())

        src_v = src.rearrange("b (t p) d -> b p t d", p=P)
        dst_v = dst.rearrange("b (t p) d -> b p t d", p=P)

        def schedule(eng, slot):
            for g in (2, 3):
                slot(At(0, -2), g)
            for c in range(-1, 3):
                for g in range(4):
                    slot(At(0, c), g)
            with eng.Fori(0, (B - 6) // 2) as k:
                for c in (3, 4):
                    for g in range(4):
                        slot(At(k, c), g)
            for c in range(B - 3, B + 1):
                for g in range(4):
                    slot(At(0, c), g)
            slot(At(0, B + 1), 0)

        def group(G):
            return not isinstance(G, int) or 0 <= G < B * 4

        def sample(s):
            return not isinstance(s.b, int) or 0 <= s.b < B

        def of_group(s, g, lag):
            return s + (g - lag) // 4, (g - lag) % 4

        @block.sync
        def _(sp):
            sp.dma_start(cos_t[:], cos).then_inc(tables_loaded, 16)
            sp.dma_start(sin_t[:], sin).then_inc(tables_loaded, 16)

            def read_stack(stack, heads, part, rows):
                for par in range(2):
                    for at, lo in enumerate(rows):
                        img = image[2 * part + lo].rearrange("(j a r) n -> a r j n", a=2, r=DH)[par]
                        sp.dma_start(stack[64 * par + DH * at:64 * par + DH * at + DH, heads(par), :], img).then_inc(
                            k_stacked if part else q_stacked, 16)

            def slot(s, g):
                G = 4 * s.b + g
                if isinstance(G, int) and G == FIRST_SLOT + 1:
                    sp.wait_ge(stacks_zeroed, 6)
                    for i in range(2):
                        for par in range(2):
                            sp.dma_start(k_stack[i][64 * par + 48:64 * par + 49, :, :], ones[:]).then_inc(stacks_set, 16)
                    sp.wait_ge(stacks_set, 64)
                if group(G - 1):
                    ps, pg = of_group(s, g, 1)
                    hold(sp, issue, mt_copied, G)
                    for a in range(GH):
                        row = q_stack[ps.par][64 * (a % 2) + 48:64 * (a % 2) + 49, GH * pg + a, :]
                        sp.dma_start(row.rearrange("p (i n) -> p i n", i=NT), mneg[(g - 1) % 2][NT * a:NT * (a + 1), :]).then_inc(rows_set[(g - 1) % 2], 16)
                if g == 0 and sample(s + -2):
                    n = s + -2
                    hold(sp, issue, res_done, 2 * n.b + 2)
                    sp.dma_start(dst_v[bass.ds(n.b, 1)].rearrange("b p t d -> p (b t) d"),
                                 res[n.par][:]).then_inc(stored[n.par], 16)
                if g == 0 and sample(s + -1):
                    n = s + -1
                    hold(sp, issue, stored[n.par], 16 * n.half)
                    sp.dma_start(res[n.par][:],
                                 src_v[bass.ds(n.b, 1)].rearrange("b p t d -> p (b t) d")).then_inc(res_loaded[n.par], 16)
                if g == (1 if not isinstance(s.b, int) or s.b > -2 else 2) and sample(s + 2):
                    n = s + 2
                    hold(sp, issue, xn_done, NT * n.b)
                    sp.dma_start(x[:], src_v[bass.ds(n.b, 1)].rearrange("b p t d -> p (b t) d")).then_inc(x_loaded, 16)
                if g == 1 and sample(s + 1):
                    n = s + 1
                    hold(sp, issue, qk_lo, 4 * n.b + 2)
                    for part, t in ((0, qk.hi), (1, qk.lo)):
                        sp.dma_start(image[part].rearrange("(c p) n -> p c n", p=P), t[:, 0:2, :]).then_inc(q_written, 16)
                if g == 2 and sample(s + 1):
                    n = s + 1
                    hold(sp, issue, st_done, 40 * (n.b - 1))
                    hold(sp, issue, q_written, 32 * (n.b + 1))
                    read_stack(q_stack[n.par], lambda par: slice(par, H, 2), 0, (0, 0, 1))
                    for par in range(2):
                        sp.dma_start(q_stack[n.par][64 * par + 48:64 * par + 49, par::2, :], zeros[:]).then_inc(q_stacked, 16)
                    hold(sp, issue, qk_lo, 4 * n.b + 4)
                    for part, t in ((2, qk.hi), (3, qk.lo)):
                        sp.dma_start(image[part].rearrange("(c p) n -> p c n", p=P), t[:, 2:4, :]).then_inc(k_written, 16)
                if g == 3 and sample(s + 1):
                    n = s + 1
                    hold(sp, issue, k_written, 32 * (n.b + 1))
                    read_stack(k_stack[n.par], lambda par: slice(0, H // 2), 1, (0, 1, 0))
                    hold(sp, issue, k_stacked, 96 * (n.b + 1))
                    hold(sp, issue, q_stacked, 128 * (n.b + 1))

            schedule(sp, slot)
            for i in range(2):
                hold(sp, issue, stored[i], 16 * (B // 2))

        @block.gpsimd
        def _(pool):
            nc.gpsimd.memset(ones[:], 1.0).then_inc(stacks_zeroed, 1)
            nc.gpsimd.memset(zeros[:], 0.0).then_inc(stacks_zeroed, 1)

            def mask(G, at, ap, dims):
                pool.sem_inc(mask_starts, 1)
                nc.gpsimd.affine_select(out=ap, in_=ap, compare_op=ALU.is_ge, fill=0.0, base=0,
                                        pattern=[[0, d] for d in dims] + [[1, P]], channel_multiplier=-1).then_inc(masked, 1)

            def rope(n, t):
                idx = 4 * n.b + t
                pool.wait_ge(rope_in, idx + 1)
                nc.gpsimd.tensor_tensor(by_sin[t % 2][:], swapped[t % 2][:], sin_t[:], ALU.mult).then_inc(sin_done, 1)
                wait(pool, qk_lo, idx - 1)
                pool.wait_ge(sin_done, idx + 1)
                nc.gpsimd.tensor_tensor(rotated[t % 2][:], by_cos[t % 2][:], by_sin[t % 2][:], ALU.add).then_inc(rope_done, 1)

            pool.wait_ge(tables_loaded, 32)

            def slot(s, g):
                G = 4 * s.b + g
                if group(G - 2):
                    pool.wait_ge(exp_done, 10 * (G - 2) + 4)
                    mask(G, 0, probs[:, 0:4, 0:P], (4,))
                if g < 2 and sample(s + 1):
                    rope(s + 1, 2 * g)
                if g == 2 and sample(s + 2):
                    n = s + 2
                    pool.wait_ge(stats_done, n.b + 1)
                    nc.gpsimd.tensor_tensor(rstd[:], ve[:, 0, :], tab.minus_half[:, 0:NT], ALU.pow).then_inc(rstd_done, 1)
                    wait(pool, xT_done, NC * n.b)
                    pool.wait_ge(rstd_done, n.b + 1)
                    pool.sem_inc(xn_starts, 1)
                    for t in range(NT):
                        nc.gpsimd.tensor_scalar(xn[:, t, :], x[:, t, :], ve[:, 1, t:t + 1], rstd[:, t:t + 1],
                                                ALU.add, ALU.mult).then_inc(xn_done, 1)
                if group(G - 2):
                    pool.wait_ge(exp_done, 10 * (G - 2) + 8)
                    mask(G, 1, probs[:, 4:8, 0:P], (4,))
                    mask(G, 2, probs[:, 4:8, 3 * P:4 * P], (4,))
                    pool.wait_ge(exp_done, 10 * (G - 2) + 10)
                    mask(G, 3, probs[:, 8:10, :].rearrange("p c (a n) -> p (c a) n", a=2)[:, :, 0:P], (4,))
                if g < 2 and sample(s + 1):
                    rope(s + 1, 2 * g + 1)
            schedule(pool, slot)

        @block.vector
        def _(dve):
            for i in range(2):
                nc.vector.memset(v[i][:], 1.0).then_inc(consts_set, 1)

            def begin_rope(n, t):
                idx = 4 * n.b + t
                dve.wait_ge(qk_done, idx + 1)
                wait(dve, rope_done, idx - 1)
                nc.vector.tensor_tensor(by_cos[t % 2][:], x_ps[t % 2][:], cos_t[:], ALU.mult)
                nc.vector.stream_shuffle(swapped[t % 2][:], x_ps[t % 2][:], [i ^ 1 for i in range(32)]).then_inc(rope_in, 1)

            def rope_low(n, t):
                dve.wait_ge(qk_hi, 4 * n.b + t + 1)
                wait(dve, q_written if t < 2 else k_written, 32 * n.b)
                nc.vector.tensor_tensor(qk.lo[:, t, :], rotated[t % 2][:], qk.hi[:, t, :], ALU.subtract).then_inc(qk_lo, 1)

            def maxima(s, g, n):
                G = 4 * s.b + g
                dve.wait_ge(mx_done, 11 * G + n + 1)
                if n == 0:
                    wait(dve, mt_done, G - 1)
                bank = mx_ps[MX_BANK[n]]
                out = mx[g % 2]
                if n < 4:
                    o_ap, i_ap = out[:, n, 3:4], bank[:]
                elif n < 8:
                    o_ap, i_ap = out[:, n - 4, 2:3], bank[:, 0:3 * P]
                elif n < 10:
                    a = 2 * (n - 8)
                    o_ap, i_ap = out[:, a:a + 2, 1], bank[:].rearrange("p (a n) -> p a n", a=2)
                else:
                    o_ap, i_ap = out[:, :, 0], bank[:].rearrange("p (a n) -> p a n", a=4)
                nc.vector.tensor_reduce(o_ap, i_ap, AX_X, ALU.max).then_inc(max_done, 1)

            dve.wait_ge(tables_loaded, 32)
            dve.wait_ge(consts_set, 2)

            def normalise_output(s, g):
                G = 4 * s.b + g
                os, og = of_group(s, g, 3)
                turned = pv_ps[:].rearrange("p (i a d) -> p i a d", i=NT, a=GH)
                dve.wait_ge(o_turned, G - 2)
                nc.vector.reciprocal(inverse[:].rearrange("p (i a) -> p i a", i=NT), turned[:, :, :, DH]).then_inc(inverse_done, 1)
                wait(dve, oT_done, NC * (os.b - 1))
                dve.wait_ge(inverse_done, G - 2)
                for i in range(NT):
                    ins = nc.vector.tensor_tensor(
                        on[os.par][:, i, GH * DH * og:GH * DH * (og + 1)].rearrange("p (a d) -> p a d", a=GH),
                        turned[:, i, :, 0:DH],
                        inverse[:, GH * i:GH * i + GH].rearrange("p (a d) -> p a d", d=1).broadcast_to([P, GH, DH]), ALU.mult)
                ins.then_inc(on_done, 1)

            def low_of(lo, hi, n, c, hi_done, lo_done):
                dve.wait_ge(hi_done, NC * n.b + c + 1)
                nc.vector.tensor_tensor(lo[:, c, :], x_ps[c][:], hi[:, c, :], ALU.subtract).then_inc(lo_done, 1)

            def slot(s, g):
                G = 4 * s.b + g
                for n in range(11):
                    if group(G):
                        maxima(s, g, n)
                    if g in (1, 2) and sample(s + 1) and n in (0, 3):
                        rope_low(s + 1, 2 * (g - 1) + (n == 3))
                    if group(G - 3) and n == 5:
                        normalise_output(s, g)
                    if g < 2 and sample(s + 1) and n in (2, 6):
                        begin_rope(s + 1, 2 * g + (n == 6))
                    if g == 2 and sample(s + 2) and n == 1:
                        dve.wait_ge(x_loaded, 16 * ((s + 2).b + 1))
                        wait(dve, xn_done, NT * (s + 2).b)
                        layernorm_stats(nc, dve, stats_step, stats_done, (s + 2).b, x, stats, pair, ve)
                    if isinstance(G, int) and G == FIRST_SLOT and n == 2:
                        for i in range(2):
                            nc.vector.memset(q_stack[i][:], 0.0).then_inc(stacks_zeroed, 1)
                            nc.vector.memset(k_stack[i][:], 0.0).then_inc(stacks_zeroed, 1)
                    if g == 3 and sample(s + 2) and n in (1, 2):
                        low_of(xT.lo, xT.hi, s + 2, n - 1, xT_hi, xT_lo)
                    if g == 3 and sample(s + -1) and n in (5, 7):
                        low_of(oT.lo, oT.hi, s + -1, int(n == 7), oT_hi, oT_lo)
                    if g == 3 and sample(s + -1) and n == 10:
                        add_residual(s + -1, 0)
                    if g == 0 and sample(s + -2) and n == 0:
                        add_residual(s + -2, 1)

            def add_residual(n, j):
                dve.wait_ge(res_loaded[n.par], 16 * (n.half + 1))
                dve.wait_ge(o_done, 2 * n.b + j + 1)
                r = res[n.par][:, 2 * j:2 * j + 2, :]
                nc.vector.tensor_tensor(r, x_ps[j][:].rearrange("p (t d) -> p t d", t=2), r, ALU.add).then_inc(res_done, 1)

            schedule(dve, slot)

        @block.scalar
        def _(act):
            def exps(G, cs):
                for c in cs:
                    wait(act, pv_done, 4 * (G - 3) + (1 if c < 4 else 3 if c < 8 else 4))
                    act.wait_ge(st_done, 10 * (G - 2) + c + 1)
                    nc.scalar.activation(probs[:, c, :], st_ps[c % 2][:], ACT.Exp, scale=DH ** -0.5).then_inc(exp_done, 1)

            def rope_high(n, t):
                act.wait_ge(rope_done, 4 * n.b + t + 1)
                wait(act, q_written if t < 2 else k_written, 32 * n.b)
                nc.scalar.activation(qk.hi[:, t, :], rotated[t % 2][:], ACT.Copy).then_inc(qk_hi, 1)

            act.wait_ge(consts_set, 2)

            def high_of(hi, n, c, ps_done, hi_done):
                act.wait_ge(ps_done, NC * n.b + c + 1)
                nc.scalar.activation(hi[:, c, :], x_ps[c][:], ACT.Copy).then_inc(hi_done, 1)

            def slot(s, g):
                G = 4 * s.b + g
                for n in range(10):
                    if group(G - 2):
                        exps(G, [n])
                    if g in (1, 2) and sample(s + 1) and n in (0, 2):
                        rope_high(s + 1, 2 * (g - 1) + (n == 2))
                    if group(G - 1) and n == 1:
                        act.wait_ge(mt_done, G)
                        wait(act, rows_set[(g - 3) % 2], 64 * (2 * s.b + (g - 3) // 2 + 1))
                        nc.scalar.activation(mneg[(g - 1) % 2][:], mx_ps[TURN_BANK][0:NT * GH, 0:P], ACT.Copy, scale=-1.0).then_inc(mt_copied, 1)
                    if group(G - 3) and n == 3:
                        act.wait_ge(pv_done, 4 * (G - 2))
                        wait(act, o_turned, G - 3)
                        nc.scalar.activation(o32[:], pv_ps[:], ACT.Copy).then_inc(o_copied, 1)
                    if g == 3 and sample(s + 2) and n in (0, 1):
                        wait(act, v_done, 2 * (s + 2).b)
                        high_of(xT.hi, s + 2, n, xT_done, xT_hi)
                    if g == 2 and sample(s + 1) and n in (4, 7):
                        v_copy(s + 1, int(n == 7))
                    if g == 3 and sample(s + -1) and n in (4, 5):
                        wait(act, o_done, 2 * (s + -1).b)
                        high_of(oT.hi, s + -1, n - 4, oT_done, oT_hi)

            def v_copy(n, j):
                act.wait_ge(v_done, 2 * n.b + j + 1)
                wait(act, pv_done, 16 * (n.b - 1))
                for t in range(2):
                    ins = nc.scalar.activation(v[n.par][:, 2 * j + t, :, 0:DH],
                                               x_ps[j][:, t * D:(t + 1) * D].rearrange("p (h d) -> p h d", h=H), ACT.Copy)
                ins.then_inc(v_copied, 1)

            schedule(act, slot)

        @block.tensor
        def _(pe):
            def part(t, p):
                return t.hi if p == "hi" else t.lo

            def turn_maxima(s, g):
                G = 4 * s.b + g
                pe.wait_ge(max_done, 11 * G)
                nc.tensor.transpose(mx_ps[TURN_BANK][0:NT * GH, 0:P], mx[(g - 1) % 2][:].rearrange("p a i -> p (a i)"),
                                    tab.ident[:]).then_inc(mt_done, 1)

            def max_scores(s, g, n):
                G = 4 * s.b + g
                if n == 4:
                    wait(pe, mt_copied, G)
                else:
                    wait(pe, max_done, 11 * G + (-2, -1, 1, 2, None, 3, 4, 5, 6, 7, 8)[n])
                if n == 0:
                    pe.wait_ge(q_stacked, 128 * (s.b + 1))
                    pe.wait_ge(k_stacked, 96 * (s.b + 1))
                bank = mx_ps[MX_BANK[n]]
                i, heads = (3, [n]) if n < 4 else (2, [n - 4]) if n < 8 else (1, [2 * n - 16, 2 * n - 15]) if n < 10 else (0, range(4))
                w = (i + 1) * P
                for at, a in enumerate(heads):
                    h = GH * g + a
                    nc.tensor.matmul(bank[:, at * w:at * w + w], q_stack[s.par][:, h, i * P:(i + 1) * P],
                                     k_stack[s.par][:, h // 2, 0:w], start=True, stop=False)
                    ins = nc.tensor.matmul(bank[:, at * w + i * P:at * w + w], tab.identb[:], tab.mask[:], start=False, stop=True)
                ins.then_inc(mx_done, 1)

            def scores(s, g, c):
                G = 4 * s.b + g - 2
                ss, sg = of_group(s, g, 2)
                bank = st_ps[c % 2]
                wait(pe, exp_done, 10 * G + c - 1)
                if c == 0:
                    pe.wait_ge(rows_set[g % 2], 64 * (2 * s.b + (g - 2) // 2 + 1))
                h = GH * sg + (c % 4 if c < 8 else 2 * (c - 8))
                work = [(h, 0, 0, 0)] if c < 4 else [(h, 1, P, 0), (h, 3, 3 * P, 3 * P)] if c < 8 else \
                    [(h, 2, 2 * P, 0), (h + 1, 2, 2 * P, 2 * P)]
                for hh, kt, q0, col in work:
                    ins = nc.tensor.matmul(bank[:, col:col + T - q0], k_stack[ss.par][:, hh // 2, kt * P:(kt + 1) * P],
                                           q_stack[ss.par][:, hh, q0:T], start=True, stop=True)
                ins.then_inc(st_done, 1)

            def probs_v(s, g, lag, nth, kt):
                G = 4 * s.b + g - lag
                ss, sg = of_group(s, g, lag)
                if kt == 0:
                    wait(pe, on_done, G)
                    pe.wait_ge(v_copied, 2 * (ss.b + 1))
                pe.wait_ge(exp_done, 10 * G + (4, 8, 10, 8)[kt])
                pe.wait_ge(masked, 4 * G + nth + 1)
                for a in range(GH):
                    p = (probs[:, a, :], probs[:, 4 + a, 0:3 * P], probs[:, 8 + a // 2, (a % 2) * 2 * P:(a % 2) * 2 * P + 2 * P],
                         probs[:, 4 + a, 3 * P:])[kt]
                    ins = nc.tensor.matmul(pv_ps[32 * a:32 * a + 32, kt * P:T], v[ss.par][:, kt, GH * sg + a, :], p,
                                           start=(kt == 0), stop=(nth == 3), tile_position=(0, 32 * a))
                ins.then_inc(pv_done, 1)

            def project_qk(n, t, half):
                idx = 4 * n.b + t
                if t == 0 and not half:
                    pe.wait_ge(xT_lo, NC * (n.b + 1))
                if t < 2 and not half:
                    wait(pe, res_done, 2 * (n.b - 2) - 1 + t)
                if t >= 2 and not half:
                    pe.wait_ge(rope_in, idx - 1)
                for i, (wp, xp) in enumerate(TERMS):
                    ins = nc.tensor.matmul(x_ps[t % 2][:], part(tab.qkv, wp)[:, int(half), t * P:(t + 1) * P],
                                           part(xT, xp)[:, int(half), :], start=(i == 0 and not half), stop=(i == 2 and half))
                if half:
                    ins.then_inc(qk_done, 1)

            def project_v(n, t):
                if t % 2 == 0:
                    pe.wait_ge(rope_in, 4 * (n.b + 1) - 1 + t // 2)
                i = 0
                for c in range(NC):
                    for xp, wp in TERMS:
                        ins = nc.tensor.matmul(x_ps[t // 2][:, (t % 2) * D:(t % 2) * D + D], part(xT, xp)[:, c, t * P:(t + 1) * P],
                                               part(tab.qkv, wp)[:, c, 2 * D:3 * D], start=(i == 0), stop=(i == 3 * NC - 1))
                        i += 1
                if t % 2:
                    ins.then_inc(v_done, 1)

            def transposes(n):
                pe.wait_ge(xn_done, NT * (n.b + 1))
                wait(pe, v_copied, 2 * n.b)
                for c in range(NC):
                    for t in range(NT):
                        ins = nc.tensor.transpose(x_ps[c][:, t * P:(t + 1) * P], xn[:, t, c * P:(c + 1) * P], tab.ident[:])
                    ins.then_inc(xT_done, 1)

            def turn_output(s, g):
                G = 4 * s.b + g
                pe.wait_ge(o_copied, G - 2)
                for i in range(NT):
                    ins = nc.tensor.transpose(pv_ps[:, i * P:(i + 1) * P], o32[:, i * P:(i + 1) * P], tab.ident[:])
                ins.then_inc(o_turned, 1)

            def transpose_o(n, s):
                pe.wait_ge(on_done, 4 * (n.b + 1))
                if sample(s + 2):
                    pe.wait_ge(xT_lo, NC * (s.b + 3))
                elif sample(s + 1):
                    pe.wait_ge(v_copied, 2 * (s.b + 2))
                else:
                    wait(pe, res_done, 2 * n.b)
                for c in range(NC):
                    for i in range(NT):
                        ins = nc.tensor.transpose(x_ps[c][:, i * P:(i + 1) * P], on[n.par][:, i, c * P:(c + 1) * P], tab.ident[:])
                    ins.then_inc(oT_done, 1)

            def project_o(n, t):
                pe.wait_ge(oT_lo, NC * (n.b + 1))
                i = 0
                for c in range(NC):
                    for op, wp in TERMS:
                        ins = nc.tensor.matmul(x_ps[t // 2][:, (t % 2) * D:(t % 2) * D + D], part(oT, op)[:, c, t * P:(t + 1) * P],
                                               part(tab.wo, wp)[:, c, :], start=(i == 0), stop=(i == 3 * NC - 1))
                        i += 1
                if t % 2:
                    ins.then_inc(o_done, 1)

            def slot(s, g):
                G = 4 * s.b + g
                cur, run = group(G), group(G - 2)
                if isinstance(G, int) and G == 0:
                    pe.wait_ge(stacks_set, 64)
                before = group(G - 3)
                for n in range(11):
                    if run and n < 10:
                        scores(s, g, n)
                    if cur:
                        max_scores(s, g, n)
                    if n == 2 and before:
                        probs_v(s, g, 3, 1, 1)
                    if n == 1 and group(G - 1):
                        turn_maxima(s, g)
                    if n == 2 and before:
                        probs_v(s, g, 3, 2, 3)
                        probs_v(s, g, 3, 3, 2)
                    if n == 5 and before:
                        turn_output(s, g)
                    if g < 2 and sample(s + 1) and n in (0, 1, 4, 5):
                        project_qk(s + 1, 2 * g + (n > 3), half=(n in (1, 5)))
                    if g == 2 and sample(s + 1) and n in (0, 1, 4, 5):
                        project_v(s + 1, (0, 1, 4, 5).index(n))
                    if g == 3 and sample(s + 2) and n == 0:
                        transposes(s + 2)
                    if run and n == 8:
                        probs_v(s, g, 2, 0, 0)
                    if g == 3 and sample(s + -1) and n == 4:
                        transpose_o(s + -1, s)
                    if g == 3 and sample(s + -1) and n >= 9:
                        project_o(s + -1, 2 * (n - 9))
                        project_o(s + -1, 2 * (n - 9) + 1)

            schedule(pe, slot)


def program(nc, x, WqkvT, WoT, Wr, br, W1, b1T, W2, b2, cos, sin, out):
    with ExitStack() as ctx:
        sb = lambda n, s, d: ctx.enter_context(nc.sbuf_tensor(n, s, d))
        tab = Tables()
        tab.w1 = Split(sb("w1_hi", [P, E, NC * D], F16), sb("w1_lo", [P, E, NC * D], F16))
        tab.w2 = Split(sb("w2_hi", [P, E, NC * D], F16), sb("w2_lo", [P, E, NC * D], F16))
        tab.b1 = sb("b1_table", [P, E, NC], F32)
        tab.qkv = Split(sb("qkv_hi", [P, NC, 3 * D], F16), sb("qkv_lo", [P, NC, 3 * D], F16))
        tab.wo = Split(sb("wo_hi", [P, NC, D], F16), sb("wo_lo", [P, NC, D], F16))
        tab.ident = sb("ident", [P, P], F32)
        tab.identb = sb("identb", [P, P], BF16)
        tab.mask = sb("mask", [P, P], BF16)
        tab.quarter = sb("quarter", [P, D], F32)
        tab.minus_half = sb("minus_half", [P, NT], F32)
        build_tables(nc, tab, W1, W2, b1T, WqkvT, WoT)
        x1 = nc.dram_tensor("after_ffn1", (B, T, D), F32, kind="Internal").ap()
        x2 = nc.dram_tensor("after_attention", (B, T, D), F32, kind="Internal").ap()
        ffn_phase(nc, "f1", tab, x, x1, Wr, br, b2)
        attention_phase(nc, tab, x1, x2, cos, sin)
        ffn_phase(nc, "f2", tab, x2, out, Wr, br, b2)


_OUT = ((B, T, D), "float32")


def kernel(L0_attn_x, L0_attn_Wqkv, L0_attn_Wo, L0_ffn_Wr, L0_ffn_br, L0_ffn_W1, L0_ffn_b1, L0_ffn_W2, L0_ffn_b2):
    import numpy as np
    import concourse.bacc as bacc
    from concourse.bass_utils import run_bass_kernel_spmd

    freqs = np.exp(np.float32(-np.log(10000.0)) * np.arange(0, DH, 2, dtype=np.float32) / np.float32(DH)).astype(np.float32)
    angles = np.arange(T, dtype=np.float32)[None, :] * freqs[(np.arange(P) % DH) // 2][:, None]
    sign = np.where(np.arange(P) % 2 == 0, -1.0, 1.0).astype(np.float32)[:, None]
    ins = {
        "x": L0_attn_x,
        "WqkvT": np.asarray(L0_attn_Wqkv).T,
        "WoT": np.asarray(L0_attn_Wo).T,
        "Wr": L0_ffn_Wr,
        "br": L0_ffn_br,
        "W1": L0_ffn_W1,
        "b1T": np.asarray(L0_ffn_b1).reshape(E, NC, P).transpose(2, 0, 1),
        "W2": L0_ffn_W2,
        "b2": L0_ffn_b2,
        "cos": np.cos(angles).astype(np.float32),
        "sin": (np.sin(angles) * sign).astype(np.float32),
    }
    nc = bacc.Bacc("TRN2", target_bir_lowering=False, num_devices=1)
    arrays, args = {}, []
    for name, a in ins.items():
        a = np.ascontiguousarray(a)
        arrays[f"in_{name}"] = a
        args.append(nc.dram_tensor(f"in_{name}", a.shape, mybir.dt.from_np(a.dtype), kind="ExternalInput").ap())
    args.append(nc.dram_tensor("out_0", _OUT[0], mybir.dt.from_np(np.dtype(_OUT[1])), kind="ExternalOutput").ap())
    program(nc, *args)
    r = run_bass_kernel_spmd(nc, [arrays], core_ids=[0])
    return r.results[0]["out_0"]
```
